# Optimizing a Trainium2 kernel written in Bass

```python
import numpy as np
import jax
import jax.numpy as jnp

def _softmax(x, axis=-1):
    return jax.nn.softmax(x, axis=axis)

def _gelu(x):
    return jax.nn.gelu(x, approximate=True)

def _silu(x):
    return jax.nn.silu(x)

def _sigmoid(x):
    return jax.nn.sigmoid(x)

def _layernorm(x, axis=-1, eps=1e-05):
    m = jnp.mean(x, axis=axis, keepdims=True)
    v = jnp.var(x, axis=axis, keepdims=True)
    return (x - m) / jnp.sqrt(v + eps)

def _scatter_add(tgt, idx, src, axis=0):
    return tgt.at[idx].add(src)

def _segment_sum(src, seg, n):
    return jax.ops.segment_sum(src, seg, n)
kernel_name = 'mk_xattn_seq_d1_seqx_r2_b455df'

def setup_inputs(seed: int=0):
    np.random.seed(seed)
    _w = jnp.asarray

    def _rec_inputs():
        import jax
        import jax.numpy as jnp
        _rk = jax.random.key(seed)
        x = -0.0003929 + 0.9999 * jax.random.normal(jax.random.fold_in(_rk, 1), (16, 512, 512), jnp.float32)
        _lenS = 512 - jax.random.randint(jax.random.fold_in(_rk, 7), (16,), 0, max(1, 512 // 4) + 1, jnp.int32)
        _lenS2 = 512 - jax.random.randint(jax.random.fold_in(_rk, 8), (16,), 0, max(1, 512 // 4) + 1, jnp.int32)
        _ctx_768P = jax.random.normal(jax.random.fold_in(_rk, 11), (16, 16, 384), jnp.float32)
        _ctx_768c = jax.random.dirichlet(jax.random.fold_in(_rk, 511), 0.3 * jnp.ones((16,), jnp.float32), (16, 512))
        _ctx_768t = jnp.einsum('bsk,bkd->bsd', _ctx_768c, _ctx_768P)
        _ctx_768t = _ctx_768t * jax.lax.rsqrt(jnp.mean(jnp.square(_ctx_768t)) + 1e-12) * 0.953939
        ctx_768 = -5.15168e-05 + 0.999825 * (_ctx_768t + 0.3 * jax.random.normal(jax.random.fold_in(_rk, 611), (16, 512, 384), jnp.float32))
        return (x, ctx_768)
    x, ctx_768 = _rec_inputs()

    def _L0_xattn_setup():
        import jax, jax.numpy as jnp
        import numpy as np
        D_TEXT, D_AUDIO, D_HID = (512, 384, 512)
        EPS = 1e-05

        def layer_norm(x, gamma, beta):
            mu = jnp.mean(x, axis=-1, keepdims=True)
            var = jnp.mean(jnp.square(x - mu), axis=-1, keepdims=True)
            return (x - mu) * jax.lax.rsqrt(var + EPS) * gamma + beta
        key = jax.random.key(seed)
        ks = jax.random.split(key, 8)
        B, L, S = (16, 512, 1024)

        def xavier(k, shape):
            bound = np.sqrt(6.0 / (shape[0] + shape[1]))
            return jax.random.uniform(k, shape, jnp.float32, -bound, bound)
        return {'H_l': jax.random.normal(ks[0], (B, L, D_TEXT), jnp.float32), 'H_a': jax.random.normal(ks[1], (B, S, D_AUDIO), jnp.float32), 'W_text': xavier(ks[2], (D_TEXT, D_HID)), 'b_text': jnp.zeros((D_HID,), jnp.float32), 'W_audio': xavier(ks[3], (D_AUDIO, D_HID)), 'b_audio': jnp.zeros((D_HID,), jnp.float32), 'W_out': xavier(ks[4], (D_HID, D_HID)), 'b_out': jnp.zeros((D_HID,), jnp.float32), 'g1': jnp.ones((D_HID,), jnp.float32), 'beta1': jnp.zeros((D_HID,), jnp.float32), 'g2': jnp.ones((D_HID,), jnp.float32), 'beta2': jnp.zeros((D_HID,), jnp.float32), 'g_out': jnp.ones((D_HID,), jnp.float32), 'beta_out': jnp.zeros((D_HID,), jnp.float32)}
    _L0_xattn_all = _L0_xattn_setup()
    _L0_xattn_in = {k: v for k, v in _L0_xattn_all.items() if k in ('W_text', 'b_text', 'W_audio', 'b_audio', 'W_out', 'b_out', 'g1', 'beta1', 'g2', 'beta2', 'g_out', 'beta_out')}
    del _L0_xattn_all
    return {'x': x, 'ctx_768': ctx_768, 'L0_xattn_W_text': _L0_xattn_in['W_text'], 'L0_xattn_b_text': _L0_xattn_in['b_text'], 'L0_xattn_W_audio': _L0_xattn_in['W_audio'], 'L0_xattn_b_audio': _L0_xattn_in['b_audio'], 'L0_xattn_W_out': _L0_xattn_in['W_out'], 'L0_xattn_b_out': _L0_xattn_in['b_out'], 'L0_xattn_g1': _L0_xattn_in['g1'], 'L0_xattn_beta1': _L0_xattn_in['beta1'], 'L0_xattn_g2': _L0_xattn_in['g2'], 'L0_xattn_beta2': _L0_xattn_in['beta2'], 'L0_xattn_g_out': _L0_xattn_in['g_out'], 'L0_xattn_beta_out': _L0_xattn_in['beta_out']}

def reference(x, ctx_768, L0_xattn_W_text, L0_xattn_b_text, L0_xattn_W_audio, L0_xattn_b_audio, L0_xattn_W_out, L0_xattn_b_out, L0_xattn_g1, L0_xattn_beta1, L0_xattn_g2, L0_xattn_beta2, L0_xattn_g_out, L0_xattn_beta_out):
    import jax
    import jax.numpy as jnp

    def _L0_xattn_ref(H_l, H_a, W_text, b_text, W_audio, b_audio, W_out, b_out, g1, beta1, g2, beta2, g_out, beta_out):
        import jax, jax.numpy as jnp
        import numpy as np
        D_TEXT, D_AUDIO, D_HID = (512, 384, 512)
        EPS = 1e-05

        def layer_norm(x, gamma, beta):
            mu = jnp.mean(x, axis=-1, keepdims=True)
            var = jnp.mean(jnp.square(x - mu), axis=-1, keepdims=True)
            return (x - mu) * jax.lax.rsqrt(var + EPS) * gamma + beta
        text_p = jnp.einsum('bld,dh->blh', H_l, W_text) + b_text
        audio_p = jnp.einsum('bsd,dh->bsh', H_a, W_audio) + b_audio
        Q = layer_norm(text_p, g1, beta1)
        K = layer_norm(audio_p, g2, beta2)
        V = audio_p
        scale = 1.0 / np.sqrt(D_HID).astype(np.float32)
        scores = jnp.einsum('blh,bsh->bls', Q, K) * scale
        alpha = jax.nn.softmax(scores, axis=-1)
        H_hyper = jnp.einsum('bls,bsh->blh', alpha, V)
        H_hyper = jnp.einsum('blh,hk->blk', H_hyper, W_out) + b_out
        return layer_norm(H_hyper + H_l, g_out, beta_out)
    x = _L0_xattn_ref(x, ctx_768, L0_xattn_W_text, L0_xattn_b_text, L0_xattn_W_audio, L0_xattn_b_audio, L0_xattn_W_out, L0_xattn_b_out, L0_xattn_g1, L0_xattn_beta1, L0_xattn_g2, L0_xattn_beta2, L0_xattn_g_out, L0_xattn_beta_out)
    return x

_drawn_inputs = setup_inputs


def setup_inputs(seed=0):
    import zlib

    import numpy as np

    out = dict(_drawn_inputs(seed))
    spreads = {'L0_xattn_b_text': (0.0, 0.521),
     'L0_xattn_b_audio': (0.0, 0.1),
     'L0_xattn_b_out': (0.0, 0.1),
     'L0_xattn_g1': (1.0, 0.2),
     'L0_xattn_beta1': (0.0, 0.511),
     'L0_xattn_g2': (1.0, 0.2),
     'L0_xattn_beta2': (0.0, 0.8),
     'L0_xattn_g_out': (1.0, 0.2),
     'L0_xattn_beta_out': (0.0, 0.1)}
    factors = {}
    for name, (base, spread) in spreads.items():
        noise = np.random.default_rng([zlib.crc32(name.encode()), seed]).standard_normal(out[name].shape)
        drawn = base * np.exp(spread * noise) if base else spread * noise
        out[name] = jnp.asarray(drawn.astype(out[name].dtype))
    for name, factor in factors.items():
        out[name] = (out[name] * factor).astype(out[name].dtype)
    return out
```

```python
import concourse.bass as bass
from concourse import mybir
from contextlib import ExitStack


def cross_attention(nc, x_rows, x_cols, ctx_rows, ctx_cols, w_text, b_text, w_audio, w_audio_t, b_audio, b_audio_col,
                    w_out, b_out, g1, beta1, g2, beta2, g_out, beta_out, out):
    f32 = mybir.dt.float32
    f32r = mybir.dt.float32r
    ALU = mybir.AluOpType
    ACT = mybir.ActivationFunctionType
    AX = mybir.AxisListType

    P = 128
    BATCHES, _, ROWS_H = x_rows.shape
    H = w_out.shape[1]
    D = w_audio.shape[0]
    T = ROWS_H // H
    L = T * P
    KH = H // P
    KD = D // P
    assert T == 4 and KH == 4 and L == 512
    SCALE = float(H) ** -0.5
    EPS = 1e-5
    DMA = 16

    def done(b, per_batch, i):
        return b * per_batch + (i + 1)

    ctx = ExitStack()
    with ctx:
        def sb(name, shape, dt=f32):
            return ctx.enter_context(nc.sbuf_tensor(name, shape, dt))

        def sem(name):
            return ctx.enter_context(nc.semaphore(name))

        wt_hi, wt_lo = sb("wt_hi", [P, KH, H], f32r), sb("wt_lo", [P, KH, H], f32r)
        wa_hi, wa_lo = sb("wa_hi", [P, KD, H], f32r), sb("wa_lo", [P, KD, H], f32r)
        wv_hi, wv_lo = sb("wv_hi", [P, KD, H], f32r), sb("wv_lo", [P, KD, H], f32r)
        bt_row, ba_row = sb("bt_row", [P, H]), sb("ba_row", [P, H])
        res_row = sb("res_row", [P, H])
        go_row, be_row = sb("go_row", [P, H]), sb("be_row", [P, H])
        cols = sb("cols", [P, 5, KH])
        G1, BETA1, G2, BETA2, BA = range(5)
        ident = sb("ident", [P, P])
        consts = sb("consts", [P, 4, T])
        MINUS_HALF, INV_H, EPSILON, ZERO = (consts[:, i, :] for i in range(4))
        w_mean = sb("w_mean", [P, KH + KD + 2])

        xT_in, cT_in = sb("xT_in", [P, KH, L]), sb("cT_in", [P, KD, L])
        c_in = sb("c_in", [P, T, D])
        y = sb("y", [P, T, H])
        xT_hi, xT_lo = sb("xT_hi", [P, KH, L], f32r), sb("xT_lo", [P, KH, L], f32r)
        cT_hi, cT_lo = sb("cT_hi", [P, KD, L], f32r), sb("cT_lo", [P, KD, L], f32r)
        c_hi, c_lo = sb("c_hi", [P, T, D], f32r), sb("c_lo", [P, T, D], f32r)

        q_rows, k_rows = sb("q_rows", [P, T, H]), sb("k_rows", [P, T, H])
        work = sb("work", [P, KH, L])
        squares_out = sb("squares_out", [P, 2, H], mybir.dt.bfloat16)
        qT_hi, qT_lo = sb("qT_hi", [P, KH, L], f32r), sb("qT_lo", [P, KH, L], f32r)
        kT_hi, kT_lo = sb("kT_hi", [P, KH, L], f32r), sb("kT_lo", [P, KH, L], f32r)
        pT_hi, pT_lo = sb("pT_hi", [P, T, L], f32r), sb("pT_lo", [P, T, L], f32r)
        pcT_hi, pcT_lo = sb("pcT_hi", [P, KD, L], f32r), sb("pcT_lo", [P, KD, L], f32r)

        q_sq, q_var, q_rstd = sb("q_sq", [P, T]), sb("q_var", [P, T]), sb("q_rstd", [P, T])
        k_sq, k_var, k_rstd = sb("k_sq", [P, T]), sb("k_var", [P, T]), sb("k_rstd", [P, T])
        s_max, s_bias = sb("s_max", [P, T]), sb("s_bias", [P, T])
        p_sum, p_inv = sb("p_sum", [P, T]), sb("p_inv", [P, T])
        y_bn, y_mv = sb("y_bn", [P, T, 6]), sb("y_mv", [P, T, 2])
        y_var, y_rstd = sb("y_var", [P, T]), sb("y_rstd", [P, T])
        y_mr, y_bias = sb("y_mr", [P, T]), sb("y_bias", [P, T])

        bank = [ctx.enter_context(nc.psum_tensor(f"bank{i}", [P, 512], f32)) for i in range(8)]
        A, B = bank[0:4], bank[4:8]

        wt_in, wa_in = q_rows, k_rows[:, 0:KD, :]
        wo_in, waT_in = work[:, :, :], c_in[:, :, :]
        ba_cols = y[:, :, 0:P]

        s_wt, s_wa, s_wo, s_waT = sem("wt_landed"), sem("wa_landed"), sem("wo_landed"), sem("waT_landed")
        s_rows = sem("rows_landed")
        s_cols = sem("cols_landed")
        s_const = sem("constants_made")
        s_ident0 = sem("identity_cleared")
        s_wmean = sem("weight_means")
        s_wcent = sem("weights_centred")
        s_wthi, s_wtlo = sem("wt_hi_made"), sem("wt_lo_made")
        s_wahi, s_walo = sem("wa_hi_made"), sem("wa_lo_made")
        s_bacols = sem("ba_cols_made")
        s_wvmm, s_resmm = sem("wv_product"), sem("res_product")
        s_wvhi, s_wvlo, s_res = sem("wv_hi_made"), sem("wv_lo_made"), sem("res_row_made")

        s_xTin, s_cTin, s_cin, s_xin = sem("xT_landed"), sem("cT_landed"), sem("c_landed"), sem("x_landed")
        s_xThi, s_xTlo = sem("xT_hi_made"), sem("xT_lo_made")
        s_cThi, s_cTlo = sem("cT_hi_made"), sem("cT_lo_made")
        s_chi, s_clo = sem("c_hi_made"), sem("c_lo_made")
        s_xres = sem("x_plus_res")
        s_tmm, s_tc, s_tsq, s_tvar, s_trs, s_qn = (
            sem("text_product"), sem("text_centred"), sem("text_squares"), sem("q_var_made"),
            sem("q_rstd_made"), sem("q_normed"))
        s_amm, s_ac, s_asq, s_avar, s_ars, s_kn = (
            sem("audio_product"), sem("audio_centred"), sem("audio_squares"), sem("k_var_made"),
            sem("k_rstd_made"), sem("k_normed"))
        s_qtr, s_qaff, s_qhi, s_qlo = sem("qT_in_psum"), sem("qT_affine"), sem("qT_hi_made"), sem("qT_lo_made")
        s_ktr, s_kaff, s_khi, s_klo = sem("kT_in_psum"), sem("kT_affine"), sem("kT_hi_made"), sem("kT_lo_made")
        s_smm, s_smax, s_sbias, s_exp = (
            sem("scores_product"), sem("scores_max"), sem("scores_bias"), sem("exp_made"))
        s_pinv = sem("p_inv_made")
        s_ptr, s_phi, s_plo = sem("pT_in_psum"), sem("pT_hi_made"), sem("pT_lo_made")
        s_pcmm, s_pchi, s_pclo = sem("p_ctx_product"), sem("pcT_hi_made"), sem("pcT_lo_made")
        s_omm, s_y, s_ybn, s_ymv = (
            sem("output_product"), sem("y_summed"), sem("y_bn_stats"), sem("y_mean_var"))
        s_yvar, s_yrs, s_ymr, s_ybias = sem("y_var_made"), sem("y_rstd_made"), sem("y_mr_made"), sem("y_bias_made")
        s_yn, s_yg, s_yout = sem("y_normed"), sem("y_scaled"), sem("y_finished")
        s_stored = sem("out_stored")

        block = ctx.enter_context(nc.Block())

        @block.sync
        def _(sp):
            def load_xT(b):
                sp.dma_start(xT_in[:, :, :], x_cols[b, :, :]
                             .rearrange("p (c l) -> p c l", c=KH)).then_inc(s_xTin, DMA)

            def load_cT(b):
                sp.dma_start(cT_in[:, :, :], ctx_cols[b, :, :]
                             .rearrange("p (c l) -> p c l", c=KD)).then_inc(s_cTin, DMA)

            def load_c(b):
                sp.dma_start(c_in[:, :, :], ctx_rows[b, :, :]
                             .rearrange("p (t d) -> p t d", t=T)).then_inc(s_cin, DMA)

            def load_x(b):
                sp.dma_start(y[:, :, :], x_rows[b, :, :]
                             .rearrange("p (t h) -> p t h", t=T)).then_inc(s_xin, DMA)

            load_xT(0)
            load_cT(0)
            sp.wait_ge(s_xTlo, 1)
            load_xT(1)
            sp.wait_ge(s_cTlo, 1)
            load_cT(1)
            sp.wait_ge(s_wvmm, KD)
            load_c(0)
            sp.wait_ge(s_resmm, 1)
            load_x(0)

            def step(b, next1=True, next2=True):
                if next2:
                    sp.wait_ge(s_xTlo, done(b + 1, 1, 0))
                    load_xT(b + 2)
                    sp.wait_ge(s_cTlo, done(b + 1, 1, 0))
                    load_cT(b + 2)
                if next1:
                    sp.wait_ge(s_clo, done(b, 1, 0))
                    load_c(b + 1)
                sp.wait_ge(s_yout, done(b, T, T - 1))
                sp.dma_start(out[b, :, :].rearrange("p (t h) -> p t h", t=T), y[:, :, :]).then_inc(s_stored, DMA)
                if next1:
                    sp.wait_ge(s_stored, DMA * (b + 1))
                    load_x(b + 1)

            step(0)
            with sp.Fori(1, BATCHES - 2) as b:
                step(b)
            step(BATCHES - 2, next2=False)
            step(BATCHES - 1, next1=False, next2=False)
            sp.wait_ge(s_stored, DMA * BATCHES)

        @block.tensor
        def _(pe):
            def product(psum, pairs, chunks):
                steps = [(l, r, k) for l, r in pairs for k in range(chunks)]
                for n, (l, r, k) in enumerate(steps):
                    last = nc.tensor.matmul(psum, l(k), r(k), start=(n == 0), stop=(n == len(steps) - 1))
                return last

            def project(t, left_hi, left_lo, right_hi, right_lo, chunks, psum):
                rows = slice(t * P, (t + 1) * P)
                lh, ll = (lambda k: left_hi[:, k, rows]), (lambda k: left_lo[:, k, rows])
                rh, rl = (lambda k: right_hi[:, k, :]), (lambda k: right_lo[:, k, :])
                return product(psum, [(lh, rh), (lh, rl), (ll, rh)], chunks)

            def text(b, reused=True):
                pe.wait_ge(s_xTlo, done(b, 1, 0))
                for t in range(T):
                    if reused:
                        pe.wait_ge(s_y, done(b - 2, T, t))
                    project(t, xT_hi, xT_lo, wt_hi, wt_lo, KH, B[t][:, :]).then_inc(s_tmm, 1)

            def audio(b):
                pe.wait_ge(s_cTlo, done(b, 1, 0))
                for t in range(T):
                    pe.wait_ge(s_tc, done(b, T, t))
                    project(t, cT_hi, cT_lo, wa_hi, wa_lo, KD, B[t][:, :]).then_inc(s_amm, 1)

            def transposes(src, c, psum, ready):
                for t in range(T):
                    last = nc.tensor.transpose(psum[:, t * P:(t + 1) * P], src[:, t, c * P:(c + 1) * P], ident[:, :])
                last.then_inc(ready, 1)

            def query_t(b, reused=True):
                pe.wait_ge(s_qn, done(b, T, T - 1))
                for c in range(KH):
                    if reused:
                        pe.wait_ge(s_plo, done(b - 1, T, c))
                    transposes(q_rows, c, A[c], s_qtr)

            def key_t(b):
                pe.wait_ge(s_kn, done(b, T, T - 1))
                for c in range(KH):
                    pe.wait_ge(s_qaff, done(b, KH, c))
                    transposes(k_rows, c, A[c], s_ktr)

            def scores(b):
                pe.wait_ge(s_qlo, done(b, KH, KH - 1))
                pe.wait_ge(s_klo, done(b, KH, KH - 1))
                for t in range(T):
                    project(t, qT_hi, qT_lo, kT_hi, kT_lo, KH, A[t][:, :]).then_inc(s_smm, 1)

            def probs_t(b):
                pe.wait_ge(s_exp, done(b, T, T - 1))
                for j in range(T):
                    transposes(work, j, A[j], s_ptr)

            def probs_ctx(b, next1=True):
                pe.wait_ge(s_clo, done(b, 1, 0))
                pe.wait_ge(s_plo, done(b, T, T - 1))
                for i in range(KD):
                    if next1:
                        pe.wait_ge(s_ac, done(b + 1, T, i))
                    else:
                        pe.wait_ge(s_y, done(b - 1, T, T - 1))
                    d = slice(i * P, (i + 1) * P)
                    ch, cl = (lambda j: c_hi[:, j, d]), (lambda j: c_lo[:, j, d])
                    ph, pl = (lambda j: pT_hi[:, j, :]), (lambda j: pT_lo[:, j, :])
                    product(B[i][:, :], [(ch, ph), (cl, ph), (ch, pl)], T).then_inc(s_pcmm, 1)

            def output(b):
                pe.wait_ge(s_pclo, done(b, KD, KD - 1))
                for t in range(T):
                    project(t, pcT_hi, pcT_lo, wv_hi, wv_lo, KD, B[t][:, :]).then_inc(s_omm, 1)

            pe.wait_ge(s_wtlo, 1)
            text(0, reused=False)
            pe.wait_ge(s_walo, 1)
            audio(0)
            pe.wait_ge(s_waT, DMA)
            pe.wait_ge(s_wo, DMA)
            for i in range(KD):
                for k in range(KH):
                    last = nc.tensor.matmul(A[i][:, :], waT_in[:, k, i * P:(i + 1) * P], wo_in[:, k, :],
                                            start=(k == 0), stop=(k == KH - 1))
                last.then_inc(s_wvmm, 1)
            pe.wait_ge(s_bacols, 1)
            for k in range(KH):
                last = nc.tensor.matmul(A[3][:, :], ba_cols[:, k, 0:P], wo_in[:, k, :],
                                        start=(k == 0), stop=(k == KH - 1))
            last.then_inc(s_resmm, 1)
            pe.wait_ge(s_const, 5)
            pe.wait_ge(s_wvlo, KD)
            pe.wait_ge(s_res, 1)
            query_t(0, reused=False)
            key_t(0)

            def step(b, first=False, next1=True):
                scores(b)
                if next1:
                    text(b + 1, reused=not first)
                probs_t(b)
                if next1:
                    audio(b + 1)
                    query_t(b + 1)
                probs_ctx(b, next1)
                if next1:
                    key_t(b + 1)
                output(b)

            step(0, first=True)
            with pe.Fori(1, BATCHES - 1) as b:
                step(b)
            step(BATCHES - 1, next1=False)

        @block.scalar
        def _(act):
            act.dma_start(wt_in[:, :, :], w_text.rearrange("(c p) h -> p c h", p=P)).then_inc(s_wt, DMA)
            for row, v in ((bt_row, b_text), (ba_row, b_audio)):
                act.dma_start(row[:, :], v.rearrange("(a h) -> a h", a=1).partition_broadcast(P)).then_inc(s_rows, DMA)
            act.dma_start(wa_in, w_audio.rearrange("(c p) h -> p c h", p=P)).then_inc(s_wa, DMA)
            for i, v in enumerate((g1, beta1, g2, beta2, b_audio_col)):
                act.dma_start(cols[:, i, :], v).then_inc(s_cols, DMA)
            act.dma_start(waT_in, w_audio_t.rearrange("(c p) d -> p c d", p=P)).then_inc(s_waT, DMA)
            act.dma_start(wo_in[:, :, :], w_out.rearrange("(c p) h -> p c h", p=P)).then_inc(s_wo, DMA)
            for row, v in ((res_row, b_out), (go_row, g_out), (be_row, beta_out)):
                act.dma_start(row[:, :], v.rearrange("(a h) -> a h", a=1).partition_broadcast(P)).then_inc(s_rows, DMA)

            def cut_xT(b):
                act.wait_ge(s_xTin, DMA * (b + 1))
                nc.scalar.activation(xT_hi[:, :, :], xT_in[:, :, :], ACT.Copy).then_inc(s_xThi, 1)

            def cut_cT(b):
                act.wait_ge(s_cTin, DMA * (b + 1))
                nc.scalar.activation(cT_hi[:, :, :], cT_in[:, :, :], ACT.Copy).then_inc(s_cThi, 1)

            def cut_c(b):
                act.wait_ge(s_cin, DMA * (b + 1))
                nc.scalar.activation(c_hi[:, :, :], c_in[:, :, :], ACT.Copy).then_inc(s_chi, 1)

            def squares(b, centred, rows, sums, ready):
                for t in range(T):
                    if t >= 2:
                        act.wait_ge(ready, done(b, T, t - 2))
                    act.wait_ge(centred, done(b, T, t))
                    nc.scalar.activation(squares_out[:, t % 2, :], rows[:, t, :], ACT.Square,
                                         accum_out=sums[:, t:t + 1]).then_inc(ready, 1)

            def text_squares(b):
                squares(b, s_tc, q_rows, q_sq, s_tsq)

            def audio_squares(b):
                squares(b, s_ac, k_rows, k_sq, s_asq)

            def normed(b, rows, rstd, rstd_made, ready):
                act.wait_ge(rstd_made, done(b, 1, 0))
                for t in range(T):
                    nc.scalar.activation(rows[:, t, :], rows[:, t, :], ACT.Copy,
                                         scale=rstd[:, t:t + 1]).then_inc(ready, 1)

            def affine_t(b, in_psum, g, beta, ready, free=None):
                for c in range(KH):
                    if free is not None:
                        act.wait_ge(free, done(b, KH, c))
                    act.wait_ge(in_psum, done(b, KH, c))
                    nc.scalar.activation(work[:, c, :], A[c][:, :], ACT.Identity, scale=cols[:, g, c:c + 1],
                                         bias=cols[:, beta, c:c + 1]).then_inc(ready, 1)

            def exps(b):
                for t in range(T):
                    act.wait_ge(s_sbias, done(b, T, t))
                    nc.scalar.activation(work[:, t, :], A[t][:, :], ACT.Exp, scale=SCALE,
                                         bias=s_bias[:, t:t + 1],
                                         accum_out=p_sum[:, t:t + 1]).then_inc(s_exp, 1)

            def probs_hi(b):
                for j in range(T):
                    act.wait_ge(s_ptr, done(b, T, j))
                    nc.scalar.activation(pT_hi[:, j, :], A[j][:, :], ACT.Copy).then_inc(s_phi, 1)

            def probs_ctx_hi(b):
                for i in range(KD):
                    act.wait_ge(s_pcmm, done(b, KD, i))
                    nc.scalar.activation(pcT_hi[:, i, :], B[i][:, :], ACT.Copy).then_inc(s_pchi, 1)

            def norm_y(b):
                act.wait_ge(s_ybias, done(b, 1, 0))
                for t in range(T):
                    nc.scalar.activation(y[:, t, :], y[:, t, :], ACT.Identity, scale=y_rstd[:, t:t + 1],
                                         bias=y_bias[:, t:t + 1]).then_inc(s_yn, 1)

            cut_xT(0)
            cut_cT(0)
            act.wait_ge(s_wcent, KH)
            nc.scalar.activation(wt_hi[:, :, :], wt_in[:, :, :], ACT.Copy).then_inc(s_wthi, 1)
            act.wait_ge(s_wcent, KH + KD)
            nc.scalar.activation(wa_hi[:, :, :], wa_in, ACT.Copy).then_inc(s_wahi, 1)
            for i in range(KD):
                act.wait_ge(s_wvmm, i + 1)
                nc.scalar.activation(wv_hi[:, i, :], A[i][:, :], ACT.Copy).then_inc(s_wvhi, 1)
            text_squares(0)
            normed(0, q_rows, q_rstd, s_trs, s_qn)
            audio_squares(0)
            normed(0, k_rows, k_rstd, s_ars, s_kn)
            act.wait_ge(s_cols, 5 * DMA)
            affine_t(0, s_qtr, G1, BETA1, s_qaff)
            affine_t(0, s_ktr, G2, BETA2, s_kaff, s_qlo)
            cut_xT(1)

            def step(b, next1=True, next2=True):
                if next1:
                    cut_cT(b + 1)
                cut_c(b)
                exps(b)
                if next1:
                    text_squares(b + 1)
                probs_hi(b)
                if next1:
                    normed(b + 1, q_rows, q_rstd, s_trs, s_qn)
                    audio_squares(b + 1)
                    affine_t(b + 1, s_qtr, G1, BETA1, s_qaff)
                    normed(b + 1, k_rows, k_rstd, s_ars, s_kn)
                probs_ctx_hi(b)
                if next1:
                    affine_t(b + 1, s_ktr, G2, BETA2, s_kaff, s_qlo)
                if next2:
                    cut_xT(b + 2)
                norm_y(b)

            step(0)
            with act.Fori(1, BATCHES - 2) as b:
                step(b)
            step(BATCHES - 2, next2=False)
            step(BATCHES - 1, next1=False, next2=False)

        @block.vector
        def _(dve):
            def f(ap):
                return ap.bitcast(f32)

            def centre(w, c, col, landed, landed_at):
                dve.wait_ge(landed, landed_at)
                nc.vector.reduce_sum(w_mean[:, col:col + 1], w, AX.X).then_inc(s_wmean, 1)
                dve.wait_ge(s_wmean, 2 * col + 1)
                nc.vector.tensor_scalar(w_mean[:, col:col + 1], w_mean[:, col:col + 1], -1.0 / H, None,
                                        ALU.mult).then_inc(s_wmean, 1)
                dve.wait_ge(s_wmean, 2 * col + 2)
                nc.vector.tensor_scalar(w, w, w_mean[:, col:col + 1], None, ALU.add).then_inc(s_wcent, 1)

            def cut_xT(b):
                dve.wait_ge(s_xThi, done(b, 1, 0))
                nc.vector.tensor_tensor(xT_lo[:, :, :], xT_in[:, :, :], f(xT_hi[:, :, :]),
                                        ALU.subtract).then_inc(s_xTlo, 1)

            def cut_cT(b):
                dve.wait_ge(s_cThi, done(b, 1, 0))
                nc.vector.tensor_tensor(cT_lo[:, :, :], cT_in[:, :, :], f(cT_hi[:, :, :]),
                                        ALU.subtract).then_inc(s_cTlo, 1)

            def cut_c(b):
                dve.wait_ge(s_chi, done(b, 1, 0))
                nc.vector.tensor_tensor(c_lo[:, :, :], c_in[:, :, :], f(c_hi[:, :, :]),
                                        ALU.subtract).then_inc(s_clo, 1)

            def add_bias(b, product, rows, bias, ready):
                for t in range(T):
                    dve.wait_ge(product, done(b, T, t))
                    nc.vector.tensor_tensor(rows[:, t, :], B[t][:, :], bias[:, :], ALU.add).then_inc(ready, 1)

            def score_max(b, t):
                dve.wait_ge(s_smm, done(b, T, t))
                nc.vector.reduce_max(s_max[:, t:t + 1], A[t][:, :], AX.X).then_inc(s_smax, 1)
                dve.wait_ge(s_smax, done(b, T, t))
                nc.vector.tensor_scalar(s_bias[:, t:t + 1], s_max[:, t:t + 1], -SCALE, None,
                                        ALU.mult).then_inc(s_sbias, 1)

            def inverse_sums(b):
                dve.wait_ge(s_exp, done(b, T, T - 1))
                nc.vector.reciprocal(p_inv[:, :], p_sum[:, :]).then_inc(s_pinv, 1)

            def cut_transposed(b, made, hi_made, lo_made, hi, lo):
                for c in range(KH + 1):
                    if c < KH:
                        dve.wait_ge(made, done(b, KH, c))
                        nc.vector.tensor_copy(hi[:, c, :], work[:, c, :]).then_inc(hi_made, 1)
                    if c:
                        dve.wait_ge(hi_made, done(b, KH, c - 1))
                        nc.vector.tensor_tensor(lo[:, c - 1, :], work[:, c - 1, :], f(hi[:, c - 1, :]),
                                                ALU.subtract).then_inc(lo_made, 1)

            def probs_lo(b):
                for j in range(T):
                    dve.wait_ge(s_phi, done(b, T, j))
                    nc.vector.tensor_tensor(pT_lo[:, j, :], A[j][:, :], f(pT_hi[:, j, :]),
                                            ALU.subtract).then_inc(s_plo, 1)

            def probs_ctx_lo(b):
                for i in range(KD):
                    dve.wait_ge(s_pchi, done(b, KD, i))
                    nc.vector.tensor_tensor(pcT_lo[:, i, :], B[i][:, :], f(pcT_hi[:, i, :]),
                                            ALU.subtract).then_inc(s_pclo, 1)

            def output_rows(b):
                dve.wait_ge(s_xres, done(b, 1, 0))
                dve.wait_ge(s_pinv, done(b, 1, 0))
                for t in range(T):
                    dve.wait_ge(s_omm, done(b, T, t))
                    nc.vector.scalar_tensor_tensor(out=y[:, t, :], in0=B[t][:, :], scalar=p_inv[:, t:t + 1],
                                                   in1=y[:, t, :], op0=ALU.mult, op1=ALU.add).then_inc(s_y, 1)
                    dve.wait_ge(s_y, done(b, T, t))
                    nc.vector.bn_stats(y_bn[:, t, :], y[:, t, :]).then_inc(s_ybn, 1)
                    dve.wait_ge(s_walo, 1)
                    dve.wait_ge(s_ybn, done(b, T, t))
                    nc.vector.bn_aggr(y_mv[:, t, :], y_bn[:, t, :]).then_inc(s_ymv, 1)

            for c in range(KH):
                centre(wt_in[:, c, :], c, c, s_wt, DMA)
            dve.wait_ge(s_wthi, 1)
            nc.vector.tensor_tensor(wt_lo[:, :, :], wt_in[:, :, :], f(wt_hi[:, :, :]),
                                    ALU.subtract).then_inc(s_wtlo, 1)
            cut_xT(0)
            for c in range(KD):
                centre(wa_in[:, c, :], c, KH + c, s_wa, DMA)
            centre(bt_row[:, :], 0, KH + KD, s_rows, 5 * DMA)
            centre(ba_row[:, :], 0, KH + KD + 1, s_rows, 5 * DMA)
            dve.wait_ge(s_wahi, 1)
            nc.vector.tensor_tensor(wa_lo[:, :, :], wa_in, f(wa_hi[:, :, :]), ALU.subtract).then_inc(s_walo, 1)
            cut_cT(0)
            dve.wait_ge(s_cols, 5 * DMA)
            nc.vector.tensor_copy(ba_cols, cols[:, BA, :].rearrange("p (c o) -> p c o", o=1)
                                  .broadcast_to([P, KH, P])).then_inc(s_bacols, 1)
            dve.wait_ge(s_wcent, KH + KD + 2)
            dve.wait_ge(s_wtlo, 1)
            add_bias(0, s_tmm, q_rows, bt_row, s_tc)
            dve.wait_ge(s_walo, 1)
            add_bias(0, s_amm, k_rows, ba_row, s_ac)
            for i in range(KD):
                dve.wait_ge(s_wvhi, i + 1)
                nc.vector.tensor_tensor(wv_lo[:, i, :], A[i][:, :], f(wv_hi[:, i, :]),
                                        ALU.subtract).then_inc(s_wvlo, 1)
            dve.wait_ge(s_resmm, 1)
            nc.vector.tensor_tensor(res_row[:, :], A[3][:, :], res_row[:, :], ALU.add).then_inc(s_res, 1)
            cut_transposed(0, s_qaff, s_qhi, s_qlo, qT_hi, qT_lo)
            cut_transposed(0, s_kaff, s_khi, s_klo, kT_hi, kT_lo)
            cut_xT(1)

            def step(b, next1=True, next2=True):
                score_max(b, 0)
                if next1:
                    cut_cT(b + 1)
                score_max(b, 1)
                cut_c(b)
                score_max(b, 2)
                score_max(b, 3)
                if next1:
                    add_bias(b + 1, s_tmm, q_rows, bt_row, s_tc)
                inverse_sums(b)
                probs_lo(b)
                if next1:
                    add_bias(b + 1, s_amm, k_rows, ba_row, s_ac)
                    cut_transposed(b + 1, s_qaff, s_qhi, s_qlo, qT_hi, qT_lo)
                probs_ctx_lo(b)
                if next1:
                    cut_transposed(b + 1, s_kaff, s_khi, s_klo, kT_hi, kT_lo)
                if next2:
                    cut_xT(b + 2)
                output_rows(b)

            step(0)
            with dve.Fori(1, BATCHES - 2) as b:
                step(b)
            step(BATCHES - 2, next2=False)
            step(BATCHES - 1, next1=False, next2=False)

        @block.gpsimd
        def _(pool):
            nc.gpsimd.memset(ident[:, :], 0.0).then_inc(s_ident0, 1)
            for const, value in ((MINUS_HALF, -0.5), (INV_H, 1.0 / H), (EPSILON, EPS), (ZERO, 0.0)):
                nc.gpsimd.memset(const, value).then_inc(s_const, 1)
            pool.wait_ge(s_ident0, 1)
            nc.gpsimd.affine_select(out=ident[:, :], in_=ident[:, :], compare_op=ALU.not_equal, fill=1.0,
                                    base=0, pattern=[[-1, P]], channel_multiplier=1).then_inc(s_const, 1)

            def inverse_deviation(b, sums, sums_made, var, var_made, rstd, rstd_made):
                pool.wait_ge(sums_made, done(b, T, T - 1))
                nc.gpsimd.tensor_tensor(var[:, :], sums[:, :], INV_H, ALU.mult).then_inc(var_made, 1)
                pool.wait_ge(var_made, done(b, 2, 0))
                nc.gpsimd.tensor_tensor(var[:, :], var[:, :], EPSILON, ALU.add).then_inc(var_made, 1)
                pool.wait_ge(var_made, done(b, 2, 1))
                nc.gpsimd.tensor_tensor(rstd[:, :], var[:, :], MINUS_HALF, ALU.pow).then_inc(rstd_made, 1)

            def text_deviation(b):
                inverse_deviation(b, q_sq, s_tsq, q_var, s_tvar, q_rstd, s_trs)

            def audio_deviation(b):
                inverse_deviation(b, k_sq, s_asq, k_var, s_avar, k_rstd, s_ars)

            def add_residual(b):
                pool.wait_ge(s_xin, DMA * (b + 1))
                nc.gpsimd.tensor_tensor(y[:, :, :], y[:, :, :],
                                        res_row[:, :].rearrange("p (o h) -> p o h", o=1)
                                        .broadcast_to([P, T, H]), ALU.add).then_inc(s_xres, 1)

            def finish(b):
                pool.wait_ge(s_ymv, done(b, T, T - 1))
                nc.gpsimd.tensor_tensor(y_var[:, :], y_mv[:, :, 1], EPSILON, ALU.add).then_inc(s_yvar, 1)
                pool.wait_ge(s_yvar, done(b, 1, 0))
                nc.gpsimd.tensor_tensor(y_rstd[:, :], y_var[:, :], MINUS_HALF, ALU.pow).then_inc(s_yrs, 1)
                pool.wait_ge(s_yrs, done(b, 1, 0))
                nc.gpsimd.tensor_tensor(y_mr[:, :], y_mv[:, :, 0], y_rstd[:, :], ALU.mult).then_inc(s_ymr, 1)
                pool.wait_ge(s_ymr, done(b, 1, 0))
                nc.gpsimd.tensor_tensor(y_bias[:, :], ZERO, y_mr[:, :], ALU.subtract).then_inc(s_ybias, 1)
                for t in range(T):
                    pool.wait_ge(s_yn, done(b, T, t))
                    nc.gpsimd.tensor_tensor(y[:, t, :], y[:, t, :], go_row[:, :], ALU.mult).then_inc(s_yg, 1)
                    pool.wait_ge(s_yg, done(b, T, t))
                    nc.gpsimd.tensor_tensor(y[:, t, :], y[:, t, :], be_row[:, :], ALU.add).then_inc(s_yout, 1)

            pool.wait_ge(s_const, 5)
            text_deviation(0)
            audio_deviation(0)
            pool.wait_ge(s_res, 1)
            def step(b, next1=True):
                if next1:
                    text_deviation(b + 1)
                add_residual(b)
                if next1:
                    audio_deviation(b + 1)
                finish(b)

            step(0)
            with pool.Fori(1, BATCHES - 1) as b:
                step(b)
            step(BATCHES - 1, next1=False)


def kernel(**inputs):
    import numpy as _np
    import concourse.bacc as _bacc
    from concourse import mybir as _mybir
    from concourse.bass_utils import run_bass_kernel_spmd as _run

    P = 128
    x = _np.asarray(inputs["x"])
    c = _np.asarray(inputs["ctx_768"])

    def rows(a):
        n, r, d = a.shape
        return a.reshape(n, P, (r // P) * d)

    def columns(a):
        n, r, d = a.shape
        return a.reshape(n, P, r // P, d // P, P).transpose(0, 4, 3, 2, 1).reshape(n, P, (d // P) * r)

    def column(v):
        return v.reshape(-1, P).T

    w = {k.removeprefix("L0_xattn_"): _np.asarray(v) for k, v in inputs.items()}
    given = {
        "x_rows": rows(x), "x_cols": columns(x), "ctx_rows": rows(c), "ctx_cols": columns(c),
        "w_text": w["W_text"], "b_text": w["b_text"], "w_audio": w["W_audio"], "w_audio_t": w["W_audio"].T,
        "b_audio": w["b_audio"], "w_out": w["W_out"], "b_out": w["b_out"],
        "g1": column(w["g1"]), "beta1": column(w["beta1"]), "g2": column(w["g2"]), "beta2": column(w["beta2"]),
        "b_audio_col": column(w["b_audio"]), "g_out": w["g_out"], "beta_out": w["beta_out"],
    }
    nc = _bacc.Bacc("TRN2", target_bir_lowering=False, num_devices=1)
    arrays, aps = {}, {}
    for name, a in given.items():
        a = _np.ascontiguousarray(a)
        arrays[f"in_{name}"] = a
        aps[name] = nc.dram_tensor(f"in_{name}", a.shape, _mybir.dt.from_np(a.dtype), kind="ExternalInput").ap()
    n, r, d = x.shape
    aps["out"] = nc.dram_tensor("out_rows", (n, P, (r // P) * d), _mybir.dt.float32, kind="ExternalOutput").ap()
    cross_attention(nc, **aps)
    res = _run(nc, [arrays], core_ids=[0])
    return res.results[0]["out_rows"].reshape(n, r, d)
```

```python
import concourse.bass as bass
from concourse import mybir
from contextlib import ExitStack


def cross_attention(nc, x_rows, x_cols, ctx_rows, ctx_cols, w_text, b_text, b_text_col, w_audio, w_audio_t, b_audio, b_audio_col,
                    w_out, b_out, g1, beta1, g2, beta2, g_out, beta_out, out):
    f32 = mybir.dt.float32
    f32r = mybir.dt.float32r
    ALU = mybir.AluOpType
    ACT = mybir.ActivationFunctionType
    AX = mybir.AxisListType

    P = 128
    BATCHES, _, ROWS_H = x_rows.shape
    H = w_out.shape[1]
    D = w_audio.shape[0]
    T = ROWS_H // H
    L = T * P
    KH = H // P
    KD = D // P
    assert T == 4 and KH == 4 and L == 512
    SCALE = float(H) ** -0.5
    EPS = 1e-5
    DMA = 16

    def done(b, per_batch, i):
        return b * per_batch + (i + 1)

    ctx = ExitStack()
    with ctx:
        def sb(name, shape, dt=f32):
            return ctx.enter_context(nc.sbuf_tensor(name, shape, dt))

        def sem(name):
            return ctx.enter_context(nc.semaphore(name))

        wt_hi, wt_lo = sb("wt_hi", [P, KH, H], f32r), sb("wt_lo", [P, KH, H], f32r)
        wa_hi, wa_lo = sb("wa_hi", [P, KD, H], f32r), sb("wa_lo", [P, KD, H], f32r)
        wv_hi, wv_lo = sb("wv_hi", [P, KD, H], f32r), sb("wv_lo", [P, KD, H], f32r)
        res_row = sb("res_row", [P, H])
        go_row, be_row = sb("go_row", [P, H]), sb("be_row", [P, H])
        cols = sb("cols", [P, 6, KH])
        G1, BETA1, G2, BETA2, BA, BT = range(6)
        bias_cols = sb("bias_cols", [P, 2, KH])
        ident = sb("ident", [P, P])
        ones = sb("ones", [P, P], f32r)
        same_of_32 = sb("same_of_32", [P, P])
        consts = sb("consts", [P, 4, T])
        MINUS_HALF, EPSILON, ZERO, ONE = range(4)
        w_mean = sb("w_mean", [P, KD + KH + 2])

        xT_in, cT_in = sb("xT_in", [P, KH, L]), sb("cT_in", [P, KD, L])
        c_in = sb("c_in", [P, T, D])
        y = sb("y", [P, T, H])
        xT_hi, xT_lo = sb("xT_hi", [P, KH, L], f32r), sb("xT_lo", [P, KH, L], f32r)
        cT_hi, cT_lo = sb("cT_hi", [P, KD, L], f32r), sb("cT_lo", [P, KD, L], f32r)
        c_hi, c_lo = sb("c_hi", [P, T, D], f32r), sb("c_lo", [P, T, D], f32r)

        q_raw, k_raw = sb("q_raw", [P, KH, L]), sb("k_raw", [P, KH, L])
        work = sb("work", [P, T, L])
        squares = sb("squares", [P, KH, L])
        diag_hi, diag_lo = sb("diag_hi", [P, T, P], f32r), sb("diag_lo", [P, T, P], f32r)
        qT_hi, qT_lo = sb("qT_hi", [P, KH, L], f32r), sb("qT_lo", [P, KH, L], f32r)
        kT_hi, kT_lo = sb("kT_hi", [P, KH, L], f32r), sb("kT_lo", [P, KH, L], f32r)
        pT_hi, pT_lo = sb("pT_hi", [P, T, L], f32r), sb("pT_lo", [P, T, L], f32r)
        pcT_hi, pcT_lo = cT_hi, cT_lo

        s_max, s_bias = sb("s_max", [P, T]), sb("s_bias", [P, T])
        p_sum, p_inv = sb("p_sum", [P, T]), sb("p_inv", [P, T])
        y_bn, y_mv = sb("y_bn", [P, T, 6]), sb("y_mv", [P, T, 2])
        y_var, y_rstd = sb("y_var", [P, T]), sb("y_rstd", [P, T])
        y_mr, y_bias = sb("y_mr", [P, T]), sb("y_bias", [P, T])

        bank = [ctx.enter_context(nc.psum_tensor(f"bank{i}", [P, 512], f32)) for i in range(8)]
        A, B = bank[0:4], bank[4:8]

        wt_in, wa_in = q_raw, k_raw[:, 0:KD, :]
        wo_in, waT_in = work[:, :, :], c_in[:, :, :]
        ba_cols = y[:, :, 0:P]
        ba_row, bt_row = squares[:, 0, :], squares[:, 1, :]

        s_wt = [sem(f"wt_landed{c}") for c in range(KH)]
        s_wa = [sem(f"wa_landed{c}") for c in range(KD)]
        s_xT0 = [sem(f"xT_of_batch0_landed{c}") for c in range(KH)]
        s_cT0 = [sem(f"cT_of_batch0_landed{c}") for c in range(KD)]
        s_wo, s_waT = sem("wo_landed"), sem("waT_landed")
        s_brows, s_rows = sem("projection_bias_rows_landed"), sem("output_rows_landed")
        s_ones, s_same = sem("ones_made"), sem("same_of_32_made")
        s_cols = sem("cols_landed")
        s_const = sem("constants_made")
        s_ident0 = sem("identity_cleared")
        s_wmean = sem("weight_means")
        s_bcent = sem("biases_centred")
        s_wthi, s_wtlo = sem("wt_hi_made"), sem("wt_lo_made")
        s_wahi, s_walo = sem("wa_hi_made"), sem("wa_lo_made")
        s_bacols = sem("ba_cols_made")
        s_wvmm, s_resmm = sem("wv_product"), sem("res_product")
        s_wvhi, s_wvlo, s_res = sem("wv_hi_made"), sem("wv_lo_made"), sem("res_row_made")

        s_xTin, s_cTin, s_cin, s_xin = sem("xT_landed"), sem("cT_landed"), sem("c_landed"), sem("x_landed")
        s_xThi, s_xTlo = sem("xT_hi_made"), sem("xT_lo_made")
        s_cThi, s_cTlo = sem("cT_hi_made"), sem("cT_lo_made")
        s_chi, s_clo = sem("c_hi_made"), sem("c_lo_made")
        s_xres = sem("x_plus_res")

        class Side:
            def __init__(self, name, inT, in_hi, in_lo, w_hi, w_lo, chunks, raw, hi, lo, bias, g, beta):
                self.inT, self.in_hi, self.in_lo, self.w_hi, self.w_lo = inT, in_hi, in_lo, w_hi, w_lo
                self.chunks, self.raw, self.hi, self.lo = chunks, raw, hi, lo
                self.var, self.rstd = sb(name + "_var_eps", [P, T]), sb(name + "_rstd", [P, T])
                self.folded = sb(name + "_folded", [P, L // 32])
                self.rstd_hi, self.rstd_lo = sb(name + "_rstd_hi", [P, T], f32r), sb(name + "_rstd_lo", [P, T])
                self.bias, self.g, self.beta = bias, g, beta
                self.product_made = sem(name + "_product")
                self.biased = sem(name + "_biased")
                self.squared = sem(name + "_squared")
                self.added = sem(name + "_squares_added")
                self.fold_made = sem(name + "_fold_made")
                self.summed = sem(name + "_summed")
                self.var_made = sem(name + "_var_made")
                self.rstd_made = sem(name + "_rstd_made")
                self.rstd_hi_made, self.rstd_lo_made = sem(name + "_rstd_hi_made"), sem(name + "_rstd_lo_made")
                self.diag_made = sem(name + "_diag_made")
                self.spread = sem(name + "_rstd_spread")
                self.normed = sem(name + "_normed")
                self.affine = sem(name + "_affine")
                self.hi_made, self.lo_made = sem(name + "_hi"), sem(name + "_lo")

        audio = Side("audio", cT_in, cT_hi, cT_lo, wa_hi, wa_lo, KD, k_raw, kT_hi, kT_lo, 0, G2, BETA2)
        text = Side("text", xT_in, xT_hi, xT_lo, wt_hi, wt_lo, KH, q_raw, qT_hi, qT_lo, 1, G1, BETA1)

        s_smm, s_smax, s_sbias, s_exp = (
            sem("scores_product"), sem("scores_max"), sem("scores_bias"), sem("exp_made"))
        s_pinv = sem("p_inv_made")
        s_ptr, s_phi, s_plo = sem("pT_in_psum"), sem("pT_hi_made"), sem("pT_lo_made")
        s_pcmm, s_pchi, s_pclo = sem("p_ctx_product"), sem("pcT_hi_made"), sem("pcT_lo_made")
        s_omm, s_y, s_ybn, s_ymv = (
            sem("output_product"), sem("y_summed"), sem("y_bn_stats"), sem("y_mean_var"))
        s_yvar, s_yrs, s_ymr, s_ybias = sem("y_var_made"), sem("y_rstd_made"), sem("y_mr_made"), sem("y_bias_made")
        s_yn, s_yg, s_yout = sem("y_normed"), sem("y_scaled"), sem("y_finished")
        s_stored = sem("out_stored")

        block = ctx.enter_context(nc.Block())

        @block.sync
        def _(sp):
            def load_xT(b):
                sp.dma_start(xT_in[:, :, :], x_cols[b, :, :]
                             .rearrange("p (c l) -> p c l", c=KH)).then_inc(s_xTin, DMA)

            def load_cT(b):
                sp.dma_start(cT_in[:, :, :], ctx_cols[b, :, :]
                             .rearrange("p (c l) -> p c l", c=KD)).then_inc(s_cTin, DMA)

            def load_c(b):
                sp.dma_start(c_in[:, :, :], ctx_rows[b, :, :]
                             .rearrange("p (t d) -> p t d", t=T)).then_inc(s_cin, DMA)

            def load_x(b):
                sp.dma_start(y[:, :, :], x_rows[b, :, :]
                             .rearrange("p (t h) -> p t h", t=T)).then_inc(s_xin, DMA)

            for inp, src, w, w_src, landed, w_landed, chunks in (
                    (cT_in, ctx_cols, wa_in, w_audio, s_cT0, s_wa, KD),
                    (xT_in, x_cols, wt_in, w_text, s_xT0, s_wt, KH)):
                for c in range(chunks):
                    sp.dma_start(w[:, c, :], w_src[c * P:(c + 1) * P, :]).then_inc(w_landed[c], DMA)
                    sp.dma_start(inp[:, c, :], src[0, :, c * L:(c + 1) * L]).then_inc(landed[c], DMA)
            sp.wait_ge(s_cTlo, KD)
            load_cT(1)
            sp.wait_ge(s_xTlo, KH)
            load_xT(1)
            sp.wait_ge(s_wvmm, KD)
            load_c(0)
            sp.wait_ge(s_resmm, 1)
            load_x(0)

            def step(b, next1=True, next2=True):
                if next2:
                    sp.wait_ge(s_xTlo, done(b + 1, KH, KH - 1))
                    load_xT(b + 2)
                    sp.wait_ge(s_cTlo, done(b + 1, KD, KD - 1))
                    load_cT(b + 2)
                if next1:
                    sp.wait_ge(s_clo, done(b, T, T - 1))
                    load_c(b + 1)
                if not next1:
                    for t in range(T):
                        sp.wait_ge(s_yout, done(b, T, t))
                        sp.dma_start(out[b, :, t * H:(t + 1) * H], y[:, t, :]).then_inc(s_stored, DMA)
                    return
                sp.wait_ge(s_yout, done(b, T, T - 1))
                sp.dma_start(out[b, :, :].rearrange("p (t h) -> p t h", t=T), y[:, :, :]).then_inc(s_stored, DMA)
                sp.wait_ge(s_stored, DMA * (b + 1))
                load_x(b + 1)

            step(0)
            with sp.Fori(1, BATCHES - 2) as b:
                step(b)
            step(BATCHES - 2, next2=False)
            step(BATCHES - 1, next1=False, next2=False)
            sp.wait_ge(s_stored, DMA * (BATCHES - 1 + T))

        @block.tensor
        def _(pe):
            def product(psum, pairs, chunks, before_chunk=lambda k: None, after_chunk=lambda k: None):
                for k in range(chunks):
                    before_chunk(k)
                    for n, (l, r) in enumerate(pairs):
                        last = nc.tensor.matmul(psum, l(k), r(k), start=(k == 0 and n == 0),
                                                stop=(k == chunks - 1 and n == len(pairs) - 1))
                    if k < chunks - 1:
                        after_chunk(k)
                return last

            def halves(t, left_hi, left_lo, right_hi, right_lo):
                rows = slice(t * P, (t + 1) * P)
                lh, ll = (lambda k: left_hi[:, k, rows]), (lambda k: left_lo[:, k, rows])
                rh, rl = (lambda k: right_hi[:, k, :]), (lambda k: right_lo[:, k, :])
                return [(lh, rh), (lh, rl), (ll, rh)]

            def tile_product(t, left_hi, left_lo, right_hi, right_lo, chunks, psum, before_chunk=lambda k: None):
                return product(psum, halves(t, left_hi, left_lo, right_hi, right_lo), chunks, before_chunk)

            def project_as_cut(side, banks, in_hi_made, in_lo_made, w_hi_made, w_lo_made):
                for k in range(side.chunks):
                    for n in range(3):
                        if n == 0:
                            pe.wait_ge(in_hi_made, k + 1)
                            pe.wait_ge(w_hi_made, k + 1)
                        elif n == 1:
                            pe.wait_ge(in_lo_made, k + 1)
                            pe.wait_ge(w_lo_made, k + 1)
                        for c in range(KH):
                            l, r = halves(c, side.w_hi, side.w_lo, side.in_hi, side.in_lo)[n]
                            last = nc.tensor.matmul(banks[c][:, :], l(k), r(k), start=(k == 0 and n == 0),
                                                    stop=(k == side.chunks - 1 and n == 2))
                            if k == side.chunks - 1 and n == 2:
                                last.then_inc(side.product_made, 1)

            def project(side, c, after_chunk=lambda k: None):
                product(B[c][:, :], halves(c, side.w_hi, side.w_lo, side.in_hi, side.in_lo), side.chunks,
                        after_chunk=after_chunk).then_inc(side.product_made, 1)

            def project_audio(b, reused=True):
                pe.wait_ge(s_cTlo, done(b, KD, KD - 1))
                for c in range(KH):
                    if reused:
                        pe.wait_ge(s_y, done(b - 2, T, c))
                    elif c == 0:
                        pe.wait_ge(s_wvlo, KD)
                    elif c == 3:
                        pe.wait_ge(s_res, 1)
                    project(audio, c)

            def project_text(b, c, after_chunk=lambda k: None):
                pe.wait_ge(s_xTlo, done(b, KH, KH - 1))
                pe.wait_ge(audio.biased, done(b, KH, c))
                project(text, c, after_chunk)

            def sum_partitions(side, b, bank, last_reader):
                pe.wait_ge(*last_reader)
                pe.wait_ge(side.fold_made, done(b, 2, 1))
                nc.tensor.matmul(bank[:, 0:L // 32], same_of_32[:, :], side.folded[:, :], start=True,
                                 stop=True).then_inc(side.summed, 1)

            def spread(side, b, bank):
                pe.wait_ge(side.diag_made, done(b, 2, 1))
                for diag in (diag_hi, diag_lo):
                    last = nc.tensor.matmul(bank[:, :], ones[:, :], diag[:, :, :].rearrange("p t i -> p (t i)"),
                                            start=(diag is diag_hi), stop=(diag is diag_lo))
                last.then_inc(side.spread, 1)

            def scores(b):
                pe.wait_ge(text.lo_made, done(b, KH, 0))
                def chunk(k):
                    pe.wait_ge(audio.lo_made, done(b, KH, k))
                    if k:
                        pe.wait_ge(text.lo_made, done(b, KH, k))
                for t in range(T):
                    tile_product(t, qT_hi, qT_lo, kT_hi, kT_lo, KH, A[t][:, :],
                                 chunk if t == 0 else lambda k: None).then_inc(s_smm, 1)

            def probs_t(b):
                pe.wait_ge(s_exp, done(b, T, T - 1))
                for j in range(T):
                    for t in range(T):
                        last = nc.tensor.transpose(A[j][:, t * P:(t + 1) * P], work[:, t, j * P:(j + 1) * P],
                                                   ident[:, :])
                    last.then_inc(s_ptr, 1)

            def probs_ctx(b, i, after_chunk=lambda k: None):
                pe.wait_ge(s_clo, done(b, T, T - 1))
                pe.wait_ge(s_plo, done(b, T, T - 1))
                d = slice(i * P, (i + 1) * P)
                ch, cl = (lambda j: c_hi[:, j, d]), (lambda j: c_lo[:, j, d])
                ph, pl = (lambda j: pT_hi[:, j, :]), (lambda j: pT_lo[:, j, :])
                product(A[i][:, :], [(ch, ph), (cl, ph), (ch, pl)], T, after_chunk=after_chunk).then_inc(s_pcmm, 1)

            def output(b, tiles, next1=True):
                def chunk(k):
                    pe.wait_ge(s_pclo, done(b, KD, k))
                for t in tiles:
                    if next1:
                        pe.wait_ge(text.biased, done(b + 1, KH, t))
                    else:
                        pe.wait_ge(s_y, done(b - 1, T, t))
                    tile_product(t, pcT_hi, pcT_lo, wv_hi, wv_lo, KD, B[t][:, :],
                                 chunk if t == 0 else lambda k: None).then_inc(s_omm, 1)

            project_as_cut(audio, B, s_cThi, s_cTlo, s_wahi, s_walo)
            project_as_cut(text, A, s_xThi, s_xTlo, s_wthi, s_wtlo)
            pe.wait_ge(s_waT, DMA)
            pe.wait_ge(s_wo, DMA)
            for i in range(KD):
                pe.wait_ge(audio.biased, i + 1)
                for k in range(KH):
                    last = nc.tensor.matmul(B[i][:, :], waT_in[:, k, i * P:(i + 1) * P], wo_in[:, k, :],
                                            start=(k == 0), stop=(k == KH - 1))
                last.then_inc(s_wvmm, 1)
                if i == 0:
                    sum_partitions(audio, 0, B[3], (audio.biased, KH))
                elif i == 1:
                    pe.wait_ge(s_ones, 1)
                    spread(audio, 0, B[3])
            sum_partitions(text, 0, A[3], (text.biased, KH))
            pe.wait_ge(audio.normed, KH)
            pe.wait_ge(s_bacols, 1)
            for k in range(KH):
                last = nc.tensor.matmul(B[3][:, :], ba_cols[:, k, 0:P], wo_in[:, k, :],
                                        start=(k == 0), stop=(k == KH - 1))
            last.then_inc(s_resmm, 1)
            spread(text, 0, A[3])
            pe.wait_ge(s_const, 5)

            def step(b, first=False, next1=True):
                scores(b)
                if next1:
                    project_audio(b + 1, reused=not first)
                probs_t(b)
                if not next1:
                    for i in range(KD):
                        probs_ctx(b, i)
                    output(b, range(T), next1=False)
                    return
                project_text(b + 1, 0)
                project_text(b + 1, 1)
                sum_partitions(audio, b + 1, A[3], (s_plo, done(b, T, T - 1)))
                project_text(b + 1, 2)
                project_text(b + 1, 3, lambda k: k == 0 and spread(audio, b + 1, A[3]))
                probs_ctx(b, 0)
                probs_ctx(b, 1, lambda k: k == 2 and sum_partitions(
                    text, b + 1, A[3], (audio.normed, done(b + 1, KH, KH - 1))))
                probs_ctx(b, 2)
                spread(text, b + 1, A[3])
                output(b, range(T))

            step(0, first=True)
            with pe.Fori(1, BATCHES - 1) as b:
                step(b)
            step(BATCHES - 1, next1=False)

        @block.scalar
        def _(act):
            def cut_xT(b, chunks):
                if 0 in chunks:
                    act.wait_ge(s_xTin, DMA * b)
                for c in chunks:
                    nc.scalar.activation(xT_hi[:, c, :], xT_in[:, c, :], ACT.Copy).then_inc(s_xThi, 1)

            def cut_cT(b):
                act.wait_ge(s_cTin, DMA * b)
                for c in range(KD):
                    nc.scalar.activation(cT_hi[:, c, :], cT_in[:, c, :], ACT.Copy).then_inc(s_cThi, 1)

            def first_hi(side, w, w_hi, w_col, landed, hi_made, w_hi_made):
                for c in range(side.chunks):
                    act.wait_ge(landed[c], DMA)
                    nc.scalar.activation(side.in_hi[:, c, :], side.inT[:, c, :], ACT.Copy).then_inc(hi_made, 1)
                    act.wait_ge(s_wmean, 2 * (w_col + c) + 2)
                    nc.scalar.activation(w_hi[:, c, :], w[:, c, :], ACT.Identity,
                                         bias=w_mean[:, w_col + c:w_col + c + 1]).then_inc(w_hi_made, 1)

            def cut_c(b):
                act.wait_ge(s_cin, DMA * (b + 1))
                for t in range(T):
                    nc.scalar.activation(c_hi[:, t, :], c_in[:, t, :], ACT.Copy).then_inc(s_chi, 1)

            def square(side, b, chunks):
                if side is text and 0 in chunks:
                    act.wait_ge(audio.fold_made, done(b, 2, 1))
                for c in chunks:
                    act.wait_ge(side.biased, done(b, KH, c))
                    nc.scalar.activation(squares[:, c, :], side.raw[:, c, :], ACT.Square).then_inc(side.squared, 1)

            def variance(side, b, bank):
                act.wait_ge(side.summed, done(b, 1, 0))
                for g in range(4):
                    group = slice(32 * g, 32 * g + 32)
                    nc.scalar.activation(side.var[group, :],
                                         bank[group, 0:L // 32].rearrange("p (t g) -> p g t", g=4)[:, g, :],
                                         ACT.Identity, scale=1.0 / H,
                                         bias=consts[group, EPSILON, 0:1]).then_inc(side.var_made, 1)

            def cut_rstd(side, b):
                act.wait_ge(side.rstd_made, done(b, 1, 0))
                nc.scalar.activation(side.rstd_hi[:, :], side.rstd[:, :], ACT.Copy).then_inc(side.rstd_hi_made, 1)

            def affine(side, b, chunks=range(KH + 1)):
                for c in chunks:
                    if c < KH:
                        act.wait_ge(side.normed, done(b, KH, c))
                        nc.scalar.activation(side.raw[:, c, :], side.raw[:, c, :], ACT.Identity,
                                             scale=cols[:, side.g, c:c + 1],
                                             bias=cols[:, side.beta, c:c + 1]).then_inc(side.affine, 1)
                    if c:
                        act.wait_ge(side.affine, done(b, KH, c - 1))
                        nc.scalar.activation(side.hi[:, c - 1, :], side.raw[:, c - 1, :],
                                             ACT.Copy).then_inc(side.hi_made, 1)

            def exps(b, tiles):
                for t in tiles:
                    act.wait_ge(s_sbias, done(b, T, t))
                    nc.scalar.activation(work[:, t, :], A[t][:, :], ACT.Exp, scale=SCALE,
                                         bias=s_bias[:, t:t + 1],
                                         accum_out=p_sum[:, t:t + 1]).then_inc(s_exp, 1)

            def probs_hi(b):
                for j in range(T):
                    act.wait_ge(s_ptr, done(b, T, j))
                    nc.scalar.activation(pT_hi[:, j, :], A[j][:, :], ACT.Copy).then_inc(s_phi, 1)

            def probs_ctx_hi(b, i):
                act.wait_ge(s_pcmm, done(b, KD, i))
                nc.scalar.activation(pcT_hi[:, i, :], A[i][:, :], ACT.Copy).then_inc(s_pchi, 1)

            def norm_y(b, by_tile=False):
                for t in range(T):
                    if by_tile or t == 0:
                        act.wait_ge(s_ybias, done(b, 1, t))
                    nc.scalar.activation(y[:, t, :], y[:, t, :], ACT.Identity, scale=y_rstd[:, t:t + 1],
                                         bias=y_bias[:, t:t + 1]).then_inc(s_yn, 1)

            first_hi(audio, wa_in, wa_hi, 0, s_cT0, s_cThi, s_wahi)
            first_hi(text, wt_in, wt_hi, KD, s_xT0, s_xThi, s_wthi)
            square(audio, 0, range(KH))
            act.wait_ge(s_const, 4)
            variance(audio, 0, B[3])
            square(text, 0, range(KH))
            cut_rstd(audio, 0)
            variance(text, 0, A[3])
            cut_rstd(text, 0)
            affine(audio, 0)
            for i in range(KD):
                act.wait_ge(s_wvmm, i + 1)
                nc.scalar.activation(wv_hi[:, i, :], B[i][:, :], ACT.Copy).then_inc(s_wvhi, 1)
            affine(text, 0)
            cut_xT(1, range(KH))

            def step(b, first=False, next1=True, next2=True):
                if next1:
                    if not first:
                        act.wait_ge(s_omm, done(b - 1, T, T - 1))
                    cut_cT(b + 1)
                exps(b, (0,))
                if not first:
                    norm_y(b - 1)
                exps(b, (1, 2, 3))
                cut_c(b)
                if next1:
                    square(audio, b + 1, range(KH))
                probs_hi(b)
                if next1:
                    variance(audio, b + 1, A[3])
                    square(text, b + 1, (0,))
                    cut_rstd(audio, b + 1)
                    square(text, b + 1, (1, 2))
                    affine(audio, b + 1, (0, 1))
                    square(text, b + 1, (3,))
                    affine(audio, b + 1, (2, 3, 4))
                probs_ctx_hi(b, 0)
                if next1:
                    variance(text, b + 1, A[3])
                probs_ctx_hi(b, 1)
                if next1:
                    cut_rstd(text, b + 1)
                probs_ctx_hi(b, 2)
                if next1:
                    affine(text, b + 1)
                if next2:
                    cut_xT(b + 2, range(KH))

            step(0, first=True)
            with act.Fori(1, BATCHES - 2) as b:
                step(b)
            step(BATCHES - 2, next2=False)
            step(BATCHES - 1, next1=False, next2=False)
            norm_y(BATCHES - 1, by_tile=True)

        @block.vector
        def _(dve):
            def f(ap):
                return ap.bitcast(f32)

            def row_mean(row, col, landed, landed_at):
                dve.wait_ge(landed, landed_at)
                nc.vector.reduce_sum(w_mean[:, col:col + 1], row, AX.X).then_inc(s_wmean, 1)
                dve.wait_ge(s_wmean, 2 * col + 1)
                nc.vector.tensor_scalar(w_mean[:, col:col + 1], w_mean[:, col:col + 1], -1.0 / H, None,
                                        ALU.mult).then_inc(s_wmean, 1)

            def first_lo(side, w, w_col, w_landed, hi_made, lo_made, w_hi_made, w_lo_made):
                for c in range(side.chunks):
                    col = w_col + c
                    row_mean(w[:, c, :], col, w_landed[c], DMA)
                    dve.wait_ge(hi_made, c + 1)
                    nc.vector.tensor_tensor(side.in_lo[:, c, :], side.inT[:, c, :], f(side.in_hi[:, c, :]),
                                            ALU.subtract).then_inc(lo_made, 1)
                    dve.wait_ge(w_hi_made, c + 1)
                    nc.vector.scalar_tensor_tensor(out=side.w_lo[:, c, :], in0=w[:, c, :],
                                                   scalar=w_mean[:, col:col + 1],
                                                   in1=f(side.w_hi[:, c, :]), op0=ALU.add,
                                                   op1=ALU.subtract).then_inc(w_lo_made, 1)

            def centre_bias(side, row, column, col):
                row_mean(row, col, s_brows, 2 * DMA)
                dve.wait_ge(s_wmean, 2 * col + 2)
                nc.vector.tensor_scalar(bias_cols[:, side.bias, :], cols[:, column, :], w_mean[:, col:col + 1], None,
                                        ALU.add).then_inc(s_bcent, 1)

            def cut_xT(b, chunks):
                for c in chunks:
                    dve.wait_ge(s_xThi, done(b, KH, c))
                    nc.vector.tensor_tensor(xT_lo[:, c, :], xT_in[:, c, :], f(xT_hi[:, c, :]),
                                            ALU.subtract).then_inc(s_xTlo, 1)

            def cut_cT(b):
                for c in range(KD):
                    dve.wait_ge(s_cThi, done(b, KD, c))
                    nc.vector.tensor_tensor(cT_lo[:, c, :], cT_in[:, c, :], f(cT_hi[:, c, :]),
                                            ALU.subtract).then_inc(s_cTlo, 1)

            def cut_c(b, t):
                dve.wait_ge(s_chi, done(b, T, t))
                nc.vector.tensor_tensor(c_lo[:, t, :], c_in[:, t, :], f(c_hi[:, t, :]),
                                        ALU.subtract).then_inc(s_clo, 1)

            def add_bias(side, b, chunks, banks=B):
                for c in chunks:
                    dve.wait_ge(side.product_made, done(b, KH, c))
                    nc.vector.tensor_scalar(side.raw[:, c, :], banks[c][:, :],
                                            bias_cols[:, side.bias, c:c + 1], None,
                                            ALU.add).then_inc(side.biased, 1)

            def fold(side, b):
                u32 = mybir.dt.uint32
                dve.wait_ge(side.added, done(b, KH - 1, KH - 2))
                nc.vector.transpose(squares[:, 1, :].bitcast(u32), squares[:, 0, :].bitcast(u32)).then_inc(side.fold_made, 1)
                dve.wait_ge(side.fold_made, done(b, 2, 0))
                nc.vector.reduce_sum(side.folded[:, :], squares[:, 1, :].rearrange("p (n i) -> p n i", i=32),
                                     AX.X).then_inc(side.fold_made, 1)

            def diagonals(side, b):
                for diag, column, made in ((diag_hi, side.rstd, side.rstd_made), (diag_lo, side.rstd_lo, side.rstd_lo_made)):
                    dve.wait_ge(made, done(b, 1, 0))
                    nc.vector.tensor_tensor(diag[:, :, :],
                                            ident[:, :].rearrange("p (o i) -> p o i", o=1).broadcast_to([P, T, P]),
                                            column[:, :].rearrange("p (t o) -> p t o", o=1).broadcast_to([P, T, P]),
                                            ALU.mult).then_inc(side.diag_made, 1)

            def norm(side, b, c, bank=A[3]):
                if c == 0:
                    dve.wait_ge(side.spread, done(b, 1, 0))
                nc.vector.tensor_tensor(side.raw[:, c, :], side.raw[:, c, :], bank[:, :],
                                        ALU.mult).then_inc(side.normed, 1)

            def cut(side, b, c):
                dve.wait_ge(side.hi_made, done(b, KH, c))
                nc.vector.tensor_tensor(side.lo[:, c, :], side.raw[:, c, :], f(side.hi[:, c, :]),
                                        ALU.subtract).then_inc(side.lo_made, 1)

            def score_max(b, t):
                dve.wait_ge(s_smm, done(b, T, t))
                nc.vector.reduce_max(s_max[:, t:t + 1], A[t][:, :], AX.X).then_inc(s_smax, 1)
                dve.wait_ge(s_smax, done(b, T, t))
                nc.vector.tensor_scalar(s_bias[:, t:t + 1], s_max[:, t:t + 1], -SCALE, None,
                                        ALU.mult).then_inc(s_sbias, 1)

            def inverse_sums(b):
                dve.wait_ge(s_exp, done(b, T, T - 1))
                nc.vector.reciprocal(p_inv[:, :], p_sum[:, :]).then_inc(s_pinv, 1)

            def probs_lo(b):
                for j in range(T):
                    dve.wait_ge(s_phi, done(b, T, j))
                    nc.vector.tensor_tensor(pT_lo[:, j, :], A[j][:, :], f(pT_hi[:, j, :]),
                                            ALU.subtract).then_inc(s_plo, 1)

            def probs_ctx_lo(b, i):
                dve.wait_ge(s_pchi, done(b, KD, i))
                nc.vector.tensor_tensor(pcT_lo[:, i, :], A[i][:, :], f(pcT_hi[:, i, :]),
                                        ALU.subtract).then_inc(s_pclo, 1)

            def scale_and_shift(b, t):
                dve.wait_ge(s_yn, done(b, T, t))
                nc.vector.tensor_tensor(y[:, t, :], y[:, t, :], go_row[:, :], ALU.mult).then_inc(s_yg, 1)
                dve.wait_ge(s_yg, done(b, T, t))
                nc.vector.tensor_tensor(y[:, t, :], y[:, t, :], be_row[:, :], ALU.add).then_inc(s_yout, 1)

            def output_rows(b, t):
                if t == 0:
                    dve.wait_ge(s_pinv, done(b, 1, 0))
                dve.wait_ge(s_xres, done(b, T, t))
                dve.wait_ge(s_omm, done(b, T, t))
                nc.vector.scalar_tensor_tensor(out=y[:, t, :], in0=B[t][:, :], scalar=p_inv[:, t:t + 1],
                                               in1=y[:, t, :], op0=ALU.mult, op1=ALU.add).then_inc(s_y, 1)
                dve.wait_ge(s_y, done(b, T, t))
                nc.vector.bn_stats(y_bn[:, t, :], y[:, t, :]).then_inc(s_ybn, 1)
                dve.wait_ge(s_walo, 1)
                dve.wait_ge(s_ybn, done(b, T, t))
                nc.vector.bn_aggr(y_mv[:, t, :], y_bn[:, t, :]).then_inc(s_ymv, 1)

            first_lo(audio, wa_in, 0, s_wa, s_cThi, s_cTlo, s_wahi, s_walo)
            first_lo(text, wt_in, KD, s_wt, s_xThi, s_xTlo, s_wthi, s_wtlo)
            dve.wait_ge(s_cols, 6 * DMA)
            centre_bias(audio, ba_row, BA, KD + KH)
            centre_bias(text, bt_row, BT, KD + KH + 1)
            dve.wait_ge(s_bcent, 2)
            dve.wait_ge(s_walo, KD)
            add_bias(audio, 0, range(KH))
            dve.wait_ge(s_wtlo, KH)
            add_bias(text, 0, range(KH), A)
            dve.wait_ge(s_const, 4)
            nc.vector.tensor_copy(ones[:, :], consts[:, ONE, 0:1].broadcast_to([P, P])).then_inc(s_ones, 1)
            nc.vector.tensor_copy(ba_cols, cols[:, BA, :].rearrange("p (c o) -> p c o", o=1)
                                  .broadcast_to([P, KH, P])).then_inc(s_bacols, 1)
            dve.wait_ge(s_const, 5)
            same = same_of_32[:, :].rearrange("p (g i) -> p g i", i=32)
            nc.vector.reduce_sum(same[:, 0, :], ident[:, :].rearrange("p (g i) -> p i g", i=32),
                                 AX.X).then_inc(s_same, 1)
            dve.wait_ge(s_same, 1)
            nc.vector.tensor_copy(same[:, 1:4, :], same[:, 0:1, :].broadcast_to([P, 3, 32])).then_inc(s_same, 1)
            dve.wait_ge(s_same, 2)
            fold(audio, 0)
            diagonals(audio, 0)
            for c in range(KH):
                norm(audio, 0, c, B[3])
            fold(text, 0)
            diagonals(text, 0)
            for c in range(KH):
                cut(audio, 0, c)
            for c in range(KH):
                norm(text, 0, c)
            for c in range(KH):
                cut(text, 0, c)
            for i in range(KD):
                dve.wait_ge(s_wvhi, i + 1)
                nc.vector.tensor_tensor(wv_lo[:, i, :], B[i][:, :], f(wv_hi[:, i, :]),
                                        ALU.subtract).then_inc(s_wvlo, 1)
            dve.wait_ge(s_rows, 3 * DMA)
            dve.wait_ge(s_resmm, 1)
            nc.vector.tensor_tensor(res_row[:, :], B[3][:, :], res_row[:, :], ALU.add).then_inc(s_res, 1)
            cut_xT(1, range(KH))

            def step(b, first=False, next1=True):
                score_max(b, 0)
                if next1:
                    cut_cT(b + 1)
                if next1 and not first:
                    cut_xT(b + 1, (0, 1))
                score_max(b, 1)
                if next1 and not first:
                    cut_xT(b + 1, (2, 3))
                score_max(b, 2)
                score_max(b, 3)
                inverse_sums(b)
                for t in range(T):
                    if next1:
                        add_bias(audio, b + 1, (t,))
                    cut_c(b, t)
                probs_lo(b)
                if next1:
                    add_bias(text, b + 1, (0,))
                    fold(audio, b + 1)
                    add_bias(text, b + 1, (1,))
                    diagonals(audio, b + 1)
                    add_bias(text, b + 1, (2,))
                    norm(audio, b + 1, 0)
                    norm(audio, b + 1, 1)
                    norm(audio, b + 1, 2)
                    add_bias(text, b + 1, (3,))
                    norm(audio, b + 1, 3)
                    cut(audio, b + 1, 0)
                    fold(text, b + 1)
                    for c in range(1, KH):
                        cut(audio, b + 1, c)
                probs_ctx_lo(b, 0)
                if next1:
                    diagonals(text, b + 1)
                probs_ctx_lo(b, 1)
                probs_ctx_lo(b, 2)
                if next1:
                    for c in range(KH):
                        norm(text, b + 1, c)
                    cut(text, b + 1, 0)
                    output_rows(b, 0)
                    cut(text, b + 1, 1)
                    cut(text, b + 1, 2)
                    output_rows(b, 1)
                    cut(text, b + 1, 3)
                    output_rows(b, 2)
                    output_rows(b, 3)
                else:
                    output_rows(b, 0)
                    for t in range(1, T):
                        output_rows(b, t)
                        scale_and_shift(b, t - 1)
                    scale_and_shift(b, T - 1)

            step(0, first=True)
            with dve.Fori(1, BATCHES - 1) as b:
                step(b)
            step(BATCHES - 1, next1=False)

        @block.gpsimd
        def _(pool):
            nc.gpsimd.memset(ident[:, :], 0.0).then_inc(s_ident0, 1)
            for const, value in ((MINUS_HALF, -0.5), (EPSILON, EPS), (ZERO, 0.0), (ONE, 1.0)):
                nc.gpsimd.memset(consts[:, const, :], value).then_inc(s_const, 1)
            for row, v in ((ba_row, b_audio), (bt_row, b_text)):
                pool.dma_start(row, v.rearrange("(a h) -> a h", a=1).partition_broadcast(P)).then_inc(s_brows, DMA)
            for i, v in enumerate((g1, beta1, g2, beta2, b_audio_col, b_text_col)):
                pool.dma_start(cols[:, i, :], v).then_inc(s_cols, DMA)
            pool.dma_start(waT_in, w_audio_t.rearrange("(c p) d -> p c d", p=P)).then_inc(s_waT, DMA)
            pool.dma_start(wo_in, w_out.rearrange("(c p) h -> p c h", p=P)).then_inc(s_wo, DMA)
            for row, v in ((res_row, b_out), (go_row, g_out), (be_row, beta_out)):
                pool.dma_start(row[:, :], v.rearrange("(a h) -> a h", a=1).partition_broadcast(P)).then_inc(s_rows, DMA)
            pool.wait_ge(s_ident0, 1)
            nc.gpsimd.affine_select(out=ident[:, :], in_=ident[:, :], compare_op=ALU.not_equal, fill=1.0,
                                    base=0, pattern=[[-1, P]], channel_multiplier=1).then_inc(s_const, 1)

            def add_squares(side, b, chunks=(1, 2, 3)):
                for c in chunks:
                    pool.wait_ge(side.squared, done(b, KH, c))
                    if c > 1:
                        pool.wait_ge(side.added, done(b, KH - 1, c - 2))
                    nc.gpsimd.tensor_tensor(squares[:, 0, :], squares[:, 0, :], squares[:, c, :],
                                            ALU.add).then_inc(side.added, 1)

            def inverse_deviation(side, b):
                pool.wait_ge(side.var_made, done(b, 4, 3))
                nc.gpsimd.tensor_tensor(side.rstd[:, :], side.var[:, :], consts[:, MINUS_HALF, :],
                                        ALU.pow).then_inc(side.rstd_made, 1)
                pool.wait_ge(side.rstd_hi_made, done(b, 1, 0))
                nc.gpsimd.tensor_tensor(side.rstd_lo[:, :], side.rstd[:, :], side.rstd_hi[:, :].bitcast(f32),
                                        ALU.subtract).then_inc(side.rstd_lo_made, 1)

            def add_residual(b, tiles):
                pool.wait_ge(s_xin, DMA * (b + 1))
                for t in tiles:
                    nc.gpsimd.tensor_tensor(y[:, t, :], y[:, t, :], res_row[:, :], ALU.add).then_inc(s_xres, 1)

            def norms(b, n, t):
                nc.gpsimd.tensor_tensor(y_var[:, t], y_mv[:, t, 1], consts[:, EPSILON, t], ALU.add).then_inc(s_yvar, 1)
                pool.wait_ge(s_yvar, done(b, 1, n))
                nc.gpsimd.tensor_tensor(y_rstd[:, t], y_var[:, t], consts[:, MINUS_HALF, t],
                                        ALU.pow).then_inc(s_yrs, 1)
                pool.wait_ge(s_yrs, done(b, 1, n))
                nc.gpsimd.tensor_tensor(y_mr[:, t], y_mv[:, t, 0], y_rstd[:, t], ALU.mult).then_inc(s_ymr, 1)
                pool.wait_ge(s_ymr, done(b, 1, n))
                nc.gpsimd.tensor_tensor(y_bias[:, t], consts[:, ZERO, t], y_mr[:, t],
                                        ALU.subtract).then_inc(s_ybias, 1)

            def finish(b):
                pool.wait_ge(s_ymv, done(b, T, T - 1))
                norms(b, 0, slice(0, T))
                for t in range(T):
                    pool.wait_ge(s_yn, done(b, T, t))
                    nc.gpsimd.tensor_tensor(y[:, t, :], y[:, t, :], go_row[:, :], ALU.mult).then_inc(s_yg, 1)
                    pool.wait_ge(s_yg, done(b, T, t))
                    nc.gpsimd.tensor_tensor(y[:, t, :], y[:, t, :], be_row[:, :], ALU.add).then_inc(s_yout, 1)

            def finish_last(b):
                for t in range(T):
                    pool.wait_ge(s_ymv, done(b, T, t))
                    norms(b, t, slice(t, t + 1))

            pool.wait_ge(s_const, 5)
            add_squares(audio, 0)
            inverse_deviation(audio, 0)
            add_squares(text, 0)
            inverse_deviation(text, 0)
            pool.wait_ge(s_res, 1)

            def step(b, first=False, next1=True):
                if not first:
                    finish(b - 1)
                if next1:
                    add_squares(audio, b + 1)
                    inverse_deviation(audio, b + 1)
                add_residual(b, (0,))
                if next1:
                    add_squares(text, b + 1)
                    inverse_deviation(text, b + 1)
                add_residual(b, (1, 2, 3))

            step(0, first=True)
            with pool.Fori(1, BATCHES - 1) as b:
                step(b)
            step(BATCHES - 1, next1=False)
            finish_last(BATCHES - 1)


def kernel(**inputs):
    import numpy as _np
    import concourse.bacc as _bacc
    from concourse import mybir as _mybir
    from concourse.bass_utils import run_bass_kernel_spmd as _run

    P = 128
    x = _np.asarray(inputs["x"])
    c = _np.asarray(inputs["ctx_768"])

    def rows(a):
        n, r, d = a.shape
        return a.reshape(n, P, (r // P) * d)

    def columns(a):
        n, r, d = a.shape
        return a.reshape(n, P, r // P, d // P, P).transpose(0, 4, 3, 2, 1).reshape(n, P, (d // P) * r)

    def column(v):
        return v.reshape(-1, P).T

    w = {k.removeprefix("L0_xattn_"): _np.asarray(v) for k, v in inputs.items()}
    given = {
        "x_rows": rows(x), "x_cols": columns(x), "ctx_rows": rows(c), "ctx_cols": columns(c),
        "w_text": w["W_text"], "b_text": w["b_text"], "w_audio": w["W_audio"], "w_audio_t": w["W_audio"].T,
        "b_audio": w["b_audio"], "w_out": w["W_out"], "b_out": w["b_out"],
        "g1": column(w["g1"]), "beta1": column(w["beta1"]), "g2": column(w["g2"]), "beta2": column(w["beta2"]),
        "b_audio_col": column(w["b_audio"]), "b_text_col": column(w["b_text"]),
        "g_out": w["g_out"], "beta_out": w["beta_out"],
    }
    nc = _bacc.Bacc("TRN2", target_bir_lowering=False, num_devices=1)
    arrays, aps = {}, {}
    for name, a in given.items():
        a = _np.ascontiguousarray(a)
        arrays[f"in_{name}"] = a
        aps[name] = nc.dram_tensor(f"in_{name}", a.shape, _mybir.dt.from_np(a.dtype), kind="ExternalInput").ap()
    n, r, d = x.shape
    aps["out"] = nc.dram_tensor("out_rows", (n, P, (r // P) * d), _mybir.dt.float32, kind="ExternalOutput").ap()
    cross_attention(nc, **aps)
    res = _run(nc, [arrays], core_ids=[0])
    return res.results[0]["out_rows"].reshape(n, r, d)
```

```python
import concourse.bass as bass
from concourse import mybir
from contextlib import ExitStack


def cross_attention(nc, x_rows, x_cols, ctx_rows, ctx_cols, w_text, b_text, b_text_col,
                    w_audio, w_audio_t, b_audio, b_audio_col, w_out, b_out, g1, beta1, g2, beta2, g_out, beta_out, out):
    f32 = mybir.dt.float32
    f32r = mybir.dt.float32r
    ALU = mybir.AluOpType
    ACT = mybir.ActivationFunctionType
    AX = mybir.AxisListType

    P = 128
    BATCHES, _, ROWS_H = x_rows.shape
    H = w_out.shape[1]
    D = w_audio.shape[0]
    T = ROWS_H // H
    L = T * P
    KH = H // P
    KD = D // P
    assert T == 4 and KH == 4 and L == 512
    SCALE = float(H) ** -0.5
    EPS = 1e-5
    DMA = 16

    def done(b, per_batch, i):
        return b * per_batch + (i + 1)

    ctx = ExitStack()
    with ctx:
        def sb(name, shape, dt=f32):
            return ctx.enter_context(nc.sbuf_tensor(name, shape, dt))

        def sem(name):
            return ctx.enter_context(nc.semaphore(name))

        wt_hi, wt_lo = sb("wt_hi", [P, KH, H], f32r), sb("wt_lo", [P, KH, H], f32r)
        wa_hi, wa_lo = sb("wa_hi", [P, KD, H], f32r), sb("wa_lo", [P, KD, H], f32r)
        wv_hi, wv_lo = sb("wv_hi", [P, KD, H], f32r), sb("wv_lo", [P, KD, H], f32r)
        res_row = sb("res_row", [P, H])
        go_row, be_row = sb("go_row", [P, H]), sb("be_row", [P, H])
        cols = sb("cols", [P, 6, KH])
        G1, BETA1, G2, BETA2, BA, BT = range(6)
        bias_cols = sb("bias_cols", [P, 2, KH])
        ident = sb("ident", [P, P])
        ones = sb("ones", [P, P], f32r)
        same_of_32 = sb("same_of_32", [P, P])
        consts = sb("consts", [P, 4, T])
        MINUS_HALF, EPSILON, ZERO, ONE = range(4)
        w_mean = sb("w_mean", [P, KD + KH + 2])

        xT_in, cT_in = sb("xT_in", [P, KH, L]), sb("cT_in", [P, KD, L])
        c_in = sb("c_in", [P, T, D])
        y = sb("y", [P, T, H])
        xT_hi, xT_lo = sb("xT_hi", [P, KH, L], f32r), sb("xT_lo", [P, KH, L], f32r)
        cT_hi, cT_lo = sb("cT_hi", [P, KD, L], f32r), sb("cT_lo", [P, KD, L], f32r)
        c_hi, c_lo = sb("c_hi", [P, T, D], f32r), sb("c_lo", [P, T, D], f32r)

        q_raw, k_raw = sb("q_raw", [P, KH, L]), sb("k_raw", [P, KH, L])
        work = sb("work", [P, T, L])
        squares = sb("squares", [P, KH, L])
        diag_hi, diag_lo = sb("diag_hi", [P, T, P], f32r), sb("diag_lo", [P, T, P], f32r)
        qT_hi, qT_lo = sb("qT_hi", [P, KH, L], f32r), sb("qT_lo", [P, KH, L], f32r)
        kT_hi, kT_lo = sb("kT_hi", [P, KH, L], f32r), sb("kT_lo", [P, KH, L], f32r)
        pT_hi, pT_lo = sb("pT_hi", [P, T, L], f32r), sb("pT_lo", [P, T, L], f32r)
        pcT_hi, pcT_lo = cT_hi, cT_lo

        s_max, s_bias = sb("s_max", [P, T]), sb("s_bias", [P, T])
        p_sum, p_inv = sb("p_sum", [P, T]), sb("p_inv", [P, T])
        y_bn, y_mv = sb("y_bn", [P, T, 6]), sb("y_mv", [P, T, 2])
        y_var, y_rstd = sb("y_var", [P, T]), sb("y_rstd", [P, T])
        y_mr, y_bias = sb("y_mr", [P, T]), sb("y_bias", [P, T])

        bank = [ctx.enter_context(nc.psum_tensor(f"bank{i}", [P, 512], f32)) for i in range(8)]
        A, B = bank[0:4], bank[4:8]

        wt_in, wa_in = q_raw, k_raw[:, 0:KD, :]
        wo_in, waT_in = work[:, :, :], c_in[:, :, :]
        ba_cols = y[:, :, 0:P]
        ba_row, bt_row = squares[:, 0, :], squares[:, 1, :]
        audio_squares0 = xT_in

        s_wt = [sem(f"wt_landed{c}") for c in range(KH)]
        s_wa = [sem(f"wa_landed{c}") for c in range(KD)]
        s_xT0 = [sem(f"xT_of_batch0_landed{c}") for c in range(KH)]
        s_cT0 = [sem(f"cT_of_batch0_landed{c}") for c in range(KD)]
        s_wo, s_waT = sem("wo_landed"), sem("waT_landed")
        s_brows, s_rows = sem("projection_bias_rows_landed"), sem("output_rows_landed")
        s_ones, s_same = sem("ones_made"), sem("same_of_32_made")
        s_cols = sem("cols_landed")
        s_const = sem("constants_made")
        s_ident0 = sem("identity_cleared")
        s_wmean = sem("weight_means")
        s_bcent = sem("biases_centred")
        s_wthi, s_wtlo = sem("wt_hi_made"), sem("wt_lo_made")
        s_wahi, s_walo = sem("wa_hi_made"), sem("wa_lo_made")
        s_bacols = sem("ba_cols_made")
        s_wvmm, s_resmm = sem("wv_product"), sem("res_product")
        s_wvhi, s_wvlo, s_res = sem("wv_hi_made"), sem("wv_lo_made"), sem("res_row_made")

        s_xTin, s_cTin, s_cin = sem("xT_landed"), sem("cT_landed"), sem("c_landed")
        s_xin = [sem(f"x_tile{t}_landed") for t in range(T)]
        s_xThi, s_xTlo = sem("xT_hi_made"), sem("xT_lo_made")
        s_cThi, s_cTlo = sem("cT_hi_made"), sem("cT_lo_made")
        s_chi, s_clo = sem("c_hi_made"), sem("c_lo_made")
        s_xres = sem("x_plus_res")

        class Side:
            def __init__(self, name, inT, in_hi, in_lo, w_hi, w_lo, chunks, raw, hi, lo, bias, g, beta):
                self.inT, self.in_hi, self.in_lo, self.w_hi, self.w_lo = inT, in_hi, in_lo, w_hi, w_lo
                self.chunks, self.raw, self.hi, self.lo = chunks, raw, hi, lo
                self.var, self.rstd = sb(name + "_var_eps", [P, T]), sb(name + "_rstd", [P, T])
                self.folded = sb(name + "_folded", [P, L // 32])
                self.rstd_hi, self.rstd_lo = sb(name + "_rstd_hi", [P, T], f32r), sb(name + "_rstd_lo", [P, T])
                self.bias, self.g, self.beta = bias, g, beta
                self.product_made = sem(name + "_product")
                self.biased = sem(name + "_biased")
                self.squared = sem(name + "_squared")
                self.added = sem(name + "_squares_added")
                self.fold_made = sem(name + "_fold_made")
                self.summed = sem(name + "_summed")
                self.var_made = sem(name + "_var_made")
                self.rstd_made = sem(name + "_rstd_made")
                self.rstd_hi_made = sem(name + "_rstd_hi_made")
                self.rstd_lo_made = sem(name + "_rstd_lo_made")
                self.diag_made = sem(name + "_diag_made")
                self.spread = sem(name + "_rstd_spread")
                self.normed = sem(name + "_normed")
                self.affine = sem(name + "_affine")
                self.hi_made, self.lo_made = sem(name + "_hi"), sem(name + "_lo")

        audio = Side("audio", cT_in, cT_hi, cT_lo, wa_hi, wa_lo, KD, k_raw, kT_hi, kT_lo, 0, G2, BETA2)
        text = Side("text", xT_in, xT_hi, xT_lo, wt_hi, wt_lo, KH, q_raw, qT_hi, qT_lo, 1, G1, BETA1)

        s_smm, s_smax, s_sbias, s_exp = (
            sem("scores_product"), sem("scores_max"), sem("scores_bias"), sem("exp_made"))
        s_pinv = sem("p_inv_made")
        s_ptr, s_phi, s_plo = sem("pT_in_psum"), sem("pT_hi_made"), sem("pT_lo_made")
        s_pcmm, s_pchi, s_pclo = sem("p_ctx_product"), sem("pcT_hi_made"), sem("pcT_lo_made")
        s_omm, s_y, s_ybn, s_ymv = (
            sem("output_product"), sem("y_summed"), sem("y_bn_stats"), sem("y_mean_var"))
        s_yvar, s_yrs, s_ymr, s_ybias = sem("y_var_made"), sem("y_rstd_made"), sem("y_mr_made"), sem("y_bias_made")
        s_yn, s_yg, s_yout = sem("y_normed"), sem("y_scaled"), sem("y_finished")
        s_yg_last, s_yout_last = sem("last_y_scaled"), sem("last_y_finished")
        s_stored = [sem(f"out_tile{t}_stored") for t in range(T)]

        block = ctx.enter_context(nc.Block())

        @block.sync
        def _(sp):
            def load_xT(b):
                sp.dma_start(xT_in[:, :, :], x_cols[b, :, :]
                             .rearrange("p (c l) -> p c l", c=KH)).then_inc(s_xTin, DMA)

            def load_cT(b):
                sp.dma_start(cT_in[:, :, :], ctx_cols[b, :, :]
                             .rearrange("p (c l) -> p c l", c=KD)).then_inc(s_cTin, DMA)

            def load_c(b):
                sp.dma_start(c_in[:, :, :], ctx_rows[b, :, :]
                             .rearrange("p (t d) -> p t d", t=T)).then_inc(s_cin, DMA)

            def load_x(b, t):
                sp.dma_start(y[:, t, :], x_rows[b, :, t * H:(t + 1) * H]).then_inc(s_xin[t], DMA)

            def store(b, t):
                sp.dma_start(out[b, :, t * H:(t + 1) * H], y[:, t, :]).then_inc(s_stored[t], DMA)

            for inp, src, w, w_src, landed, w_landed, chunks in (
                    (xT_in, x_cols, wt_in, w_text, s_xT0, s_wt, KH),
                    (cT_in, ctx_cols, wa_in, w_audio, s_cT0, s_wa, KD)):
                for c in range(chunks):
                    sp.dma_start(w[:, c, :], w_src[c * P:(c + 1) * P, :]).then_inc(w_landed[c], DMA)
                    sp.dma_start(inp[:, c, :], src[0, :, c * L:(c + 1) * L]).then_inc(landed[c], DMA)
            sp.wait_ge(s_cTlo, KD)
            load_cT(1)
            sp.wait_ge(audio.fold_made, 2)
            load_xT(1)
            sp.wait_ge(s_wvmm, KD)
            load_c(0)
            sp.wait_ge(s_resmm, 1)
            for t in range(T):
                load_x(0, t)

            def step(b, next2=True):
                if next2:
                    sp.wait_ge(s_xTlo, done(b + 1, KH, KH - 1))
                    load_xT(b + 2)
                    sp.wait_ge(s_cTlo, done(b + 1, KD, KD - 1))
                    load_cT(b + 2)
                sp.wait_ge(s_clo, done(b, T, T - 1))
                load_c(b + 1)
                for t in range(T + 1):
                    if t < T:
                        sp.wait_ge(s_yout, done(b, T, t))
                        store(b, t)
                    if t:
                        sp.wait_ge(s_stored[t - 1], DMA * (b + 1))
                        load_x(b + 1, t - 1)

            def last_stores(b):
                for t in (1, 2, 3, 0):
                    if t:
                        sp.wait_ge(s_yout_last, t)
                    else:
                        sp.wait_ge(s_yout, done(b, T, 0))
                    store(b, t)

            step(0)
            with sp.Fori(1, BATCHES - 2) as b:
                step(b)
            step(BATCHES - 2, next2=False)
            last_stores(BATCHES - 1)
            for t in range(T):
                sp.wait_ge(s_stored[t], DMA * BATCHES)

        @block.tensor
        def _(pe):
            def product(psum, pairs, chunks, before_chunk=lambda k: None, after_chunk=lambda k: None):
                for k in range(chunks):
                    before_chunk(k)
                    for n, (l, r) in enumerate(pairs):
                        last = nc.tensor.matmul(psum, l(k), r(k), start=(k == 0 and n == 0),
                                                stop=(k == chunks - 1 and n == len(pairs) - 1))
                    if k < chunks - 1:
                        after_chunk(k)
                return last

            def halves(t, left_hi, left_lo, right_hi, right_lo):
                rows = slice(t * P, (t + 1) * P)
                lh, ll = (lambda k: left_hi[:, k, rows]), (lambda k: left_lo[:, k, rows])
                rh, rl = (lambda k: right_hi[:, k, :]), (lambda k: right_lo[:, k, :])
                return [(lh, rh), (lh, rl), (ll, rh)]

            def tile_product(t, left_hi, left_lo, right_hi, right_lo, chunks, psum, before_chunk=lambda k: None):
                return product(psum, halves(t, left_hi, left_lo, right_hi, right_lo), chunks, before_chunk)

            def project_as_cut(side, banks, in_hi_made, in_lo_made, w_hi_made, w_lo_made):
                for k in range(side.chunks):
                    for n in range(3):
                        if n == 0:
                            pe.wait_ge(in_hi_made, k + 1)
                            pe.wait_ge(w_hi_made, k + 1)
                        elif n == 1:
                            pe.wait_ge(in_lo_made, k + 1)
                            pe.wait_ge(w_lo_made, k + 1)
                        for c in range(KH):
                            l, r = halves(c, side.w_hi, side.w_lo, side.in_hi, side.in_lo)[n]
                            last = nc.tensor.matmul(banks[c][:, :], l(k), r(k), start=(k == 0 and n == 0),
                                                    stop=(k == side.chunks - 1 and n == 2))
                            if k == side.chunks - 1 and n == 2:
                                last.then_inc(side.product_made, 1)

            def project(side, c, after_chunk=lambda k: None):
                product(B[c][:, :], halves(c, side.w_hi, side.w_lo, side.in_hi, side.in_lo), side.chunks,
                        after_chunk=after_chunk).then_inc(side.product_made, 1)

            def project_audio(b, reused=True):
                pe.wait_ge(s_cTlo, done(b, KD, KD - 1))
                for c in range(KH):
                    if reused:
                        pe.wait_ge(s_y, done(b - 2, T, c))
                    elif c == 0:
                        pe.wait_ge(s_wvlo, KD)
                    project(audio, c)

            def project_text(b, c, after_chunk=lambda k: None):
                pe.wait_ge(s_xTlo, done(b, KH, KH - 1))
                pe.wait_ge(audio.biased, done(b, KH, c))
                project(text, c, after_chunk)

            def sum_partitions(side, b, bank, last_reader):
                pe.wait_ge(*last_reader)
                pe.wait_ge(side.fold_made, done(b, 2, 1))
                nc.tensor.matmul(bank[:, 0:L // 32], same_of_32[:, :], side.folded[:, :], start=True,
                                 stop=True).then_inc(side.summed, 1)

            def spread(side, b, bank):
                pe.wait_ge(side.diag_made, done(b, 2, 1))
                for diag in (diag_hi, diag_lo):
                    last = nc.tensor.matmul(bank[:, :], ones[:, :], diag[:, :, :].rearrange("p t i -> p (t i)"),
                                            start=(diag is diag_hi), stop=(diag is diag_lo))
                last.then_inc(side.spread, 1)

            def set_up_product(k, left, psum, ready):
                last = nc.tensor.matmul(psum, left, wo_in[:, k, :], start=(k == 0), stop=(k == KH - 1))
                if k == KH - 1:
                    last.then_inc(ready, 1)

            def first_scores():
                def tile(t, k):
                    for n, (l, r) in enumerate(halves(t, qT_hi, qT_lo, kT_hi, kT_lo)):
                        last = nc.tensor.matmul(A[t][:, :], l(k), r(k), start=(k == 0 and n == 0),
                                                stop=(k == KH - 1 and n == 2))
                    if k == KH - 1:
                        last.then_inc(s_smm, 1)
                for k in range(KH):
                    pe.wait_ge(audio.lo_made, k + 1)
                    pe.wait_ge(text.lo_made, k + 1)
                    for t in (1, 2, 0) if k == 0 else range(T):
                        if (k, t) == (0, 0):
                            pe.wait_ge(s_res, 1)
                        elif (k, t) == (1, T - 1):
                            pe.wait_ge(audio.normed, KH)
                            tile(t, 0)
                        tile(t, k)

            def scores(b, after_tile=lambda t: None):
                pe.wait_ge(text.lo_made, done(b, KH, 0))
                def chunk(k):
                    pe.wait_ge(audio.lo_made, done(b, KH, k))
                    if k:
                        pe.wait_ge(text.lo_made, done(b, KH, k))
                for t in range(T):
                    tile_product(t, qT_hi, qT_lo, kT_hi, kT_lo, KH, A[t][:, :],
                                 chunk if t == 0 else lambda k: None).then_inc(s_smm, 1)
                    after_tile(t)

            def transpose_probs(b, t, j, bank):
                return nc.tensor.transpose(bank[:, t * P:(t + 1) * P], work[:, t, j * P:(j + 1) * P], ident[:, :])

            def probs_t(b):
                pe.wait_ge(s_exp, done(b, T, T - 1))
                for j in range(T):
                    for t in range(T):
                        last = transpose_probs(b, t, j, A[j])
                    last.then_inc(s_ptr, 1)

            def probs_t_of_tile(b, t):
                pe.wait_ge(s_y, done(b - 1, T, T - 1))
                pe.wait_ge(s_exp, done(b, T, t))
                for j in range(T):
                    last = transpose_probs(b, t, j, B[j])
                    if t == T - 1:
                        last.then_inc(s_ptr, 1)

            def probs_ctx(b, i, by_tile=False, after_chunk=lambda k: None):
                pe.wait_ge(s_clo, done(b, T, T - 1))
                def chunk(j):
                    if by_tile or j == 0:
                        pe.wait_ge(s_plo, done(b, T, j if by_tile else T - 1))
                d = slice(i * P, (i + 1) * P)
                ch, cl = (lambda j: c_hi[:, j, d]), (lambda j: c_lo[:, j, d])
                ph, pl = (lambda j: pT_hi[:, j, :]), (lambda j: pT_lo[:, j, :])
                product(A[i][:, :], [(ch, ph), (cl, ph), (ch, pl)], T, chunk, after_chunk).then_inc(s_pcmm, 1)

            def output(b, tiles, next1=True):
                def chunk(k):
                    pe.wait_ge(s_pclo, done(b, KD, k))
                for t in tiles:
                    if next1:
                        pe.wait_ge(text.biased, done(b + 1, KH, t))
                    else:
                        pe.wait_ge(s_plo, done(b, T, T - 1))
                    tile_product(t, pcT_hi, pcT_lo, wv_hi, wv_lo, KD, B[t][:, :],
                                 chunk if t == 0 else lambda k: None).then_inc(s_omm, 1)

            project_as_cut(text, B, s_xThi, s_xTlo, s_wthi, s_wtlo)
            project_as_cut(audio, A, s_cThi, s_cTlo, s_wahi, s_walo)
            pe.wait_ge(s_waT, DMA)
            pe.wait_ge(s_wo, DMA)
            for i in range(KD):
                pe.wait_ge(text.biased, i + 1)
                for k in range(KH):
                    set_up_product(k, waT_in[:, k, i * P:(i + 1) * P], B[i][:, :], s_wvmm)
                    if (i, k) == (0, 0):
                        sum_partitions(text, 0, B[3], (text.biased, KH))
                    elif (i, k) == (1, 0):
                        pe.wait_ge(s_ones, 1)
                        spread(text, 0, B[3])
                    elif (i, k) == (2, 0):
                        sum_partitions(audio, 0, A[3], (audio.biased, KH))
                    elif (i, k) == (2, 3):
                        spread(audio, 0, A[3])
            pe.wait_ge(s_bacols, 1)
            for k in range(KH):
                set_up_product(k, ba_cols[:, k, 0:P], A[0][:, :], s_resmm)
            pe.wait_ge(s_const, 5)

            def step(b, first=False):
                if first:
                    first_scores()
                else:
                    scores(b)
                project_audio(b + 1, reused=not first)
                probs_t(b)
                project_text(b + 1, 0)
                project_text(b + 1, 1)
                sum_partitions(audio, b + 1, A[3], (s_plo, done(b, T, T - 1)))
                project_text(b + 1, 2)
                project_text(b + 1, 3, lambda k: k == 0 and spread(audio, b + 1, A[3]))
                probs_ctx(b, 0)
                probs_ctx(b, 1, after_chunk=lambda k: k == 2 and sum_partitions(
                    text, b + 1, A[3], (audio.normed, done(b + 1, KH, KH - 1))))
                probs_ctx(b, 2)
                spread(text, b + 1, A[3])
                output(b, range(T))

            def last_step(b):
                scores(b, lambda t: t > 1 and probs_t_of_tile(b, t - 2))
                probs_t_of_tile(b, T - 2)
                probs_t_of_tile(b, T - 1)
                for i in range(KD):
                    probs_ctx(b, i, by_tile=True)
                output(b, range(T), next1=False)

            step(0, first=True)
            with pe.Fori(1, BATCHES - 1) as b:
                step(b)
            last_step(BATCHES - 1)

        @block.scalar
        def _(act):
            def cut_xT(b, chunks):
                if 0 in chunks:
                    act.wait_ge(s_xTin, DMA * b)
                for c in chunks:
                    nc.scalar.activation(xT_hi[:, c, :], xT_in[:, c, :], ACT.Copy).then_inc(s_xThi, 1)

            def cut_cT(b):
                act.wait_ge(s_cTin, DMA * b)
                for c in range(KD):
                    nc.scalar.activation(cT_hi[:, c, :], cT_in[:, c, :], ACT.Copy).then_inc(s_cThi, 1)

            def first_hi(side, c, w, w_hi, w_col, landed, hi_made, w_hi_made):
                act.wait_ge(landed[c], DMA)
                nc.scalar.activation(side.in_hi[:, c, :], side.inT[:, c, :], ACT.Copy).then_inc(hi_made, 1)
                act.wait_ge(s_wmean, 2 * (w_col + c) + 2)
                nc.scalar.activation(w_hi[:, c, :], w[:, c, :], ACT.Identity,
                                     bias=w_mean[:, w_col + c:w_col + c + 1]).then_inc(w_hi_made, 1)

            def cut_c(b):
                act.wait_ge(s_cin, DMA * (b + 1))
                for t in range(T):
                    nc.scalar.activation(c_hi[:, t, :], c_in[:, t, :], ACT.Copy).then_inc(s_chi, 1)

            def first_bias(side, c, banks):
                act.wait_ge(side.product_made, c + 1)
                nc.scalar.activation(side.raw[:, c, :], banks[c][:, :], ACT.Identity,
                                     bias=bias_cols[:, side.bias, c:c + 1]).then_inc(side.biased, 1)

            def first_square(side, c, squares):
                square(side, 0, (c,), squares, first=True)

            def square(side, b, chunks, squares=squares, first=False):
                if side is text and 0 in chunks and not first:
                    act.wait_ge(audio.fold_made, done(b, 2, 1))
                for c in chunks:
                    act.wait_ge(side.biased, done(b, KH, c))
                    nc.scalar.activation(squares[:, c, :], side.raw[:, c, :], ACT.Square).then_inc(side.squared, 1)

            def variance(side, b, bank):
                act.wait_ge(side.summed, done(b, 1, 0))
                for g in range(4):
                    group = slice(32 * g, 32 * g + 32)
                    nc.scalar.activation(side.var[group, :],
                                         bank[group, 0:L // 32].rearrange("p (t g) -> p g t", g=4)[:, g, :],
                                         ACT.Identity, scale=1.0 / H,
                                         bias=consts[group, EPSILON, 0:1]).then_inc(side.var_made, 1)

            def cut_rstd(side, b):
                act.wait_ge(side.rstd_made, done(b, 1, 0))
                nc.scalar.activation(side.rstd_hi[:, :], side.rstd[:, :], ACT.Copy).then_inc(side.rstd_hi_made, 1)

            def affine_chunk(side, b, c):
                act.wait_ge(side.normed, done(b, KH, c))
                nc.scalar.activation(side.raw[:, c, :], side.raw[:, c, :], ACT.Identity,
                                     scale=cols[:, side.g, c:c + 1],
                                     bias=cols[:, side.beta, c:c + 1]).then_inc(side.affine, 1)

            def cut_chunk(side, b, c):
                act.wait_ge(side.affine, done(b, KH, c))
                nc.scalar.activation(side.hi[:, c, :], side.raw[:, c, :], ACT.Copy).then_inc(side.hi_made, 1)

            def affine(side, b, chunks=range(KH + 1)):
                for c in chunks:
                    if c < KH:
                        affine_chunk(side, b, c)
                    if c:
                        cut_chunk(side, b, c - 1)

            def exps(b, tiles):
                for t in tiles:
                    act.wait_ge(s_sbias, done(b, T, t))
                    nc.scalar.activation(work[:, t, :], A[t][:, :], ACT.Exp, scale=SCALE,
                                         bias=s_bias[:, t:t + 1],
                                         accum_out=p_sum[:, t:t + 1]).then_inc(s_exp, 1)

            def probs_hi(b, banks):
                for j in range(T):
                    act.wait_ge(s_ptr, done(b, T, j))
                    nc.scalar.activation(pT_hi[:, j, :], banks[j][:, :], ACT.Copy).then_inc(s_phi, 1)

            def probs_ctx_hi(b, i):
                act.wait_ge(s_pcmm, done(b, KD, i))
                nc.scalar.activation(pcT_hi[:, i, :], A[i][:, :], ACT.Copy).then_inc(s_pchi, 1)

            def norm_y(b, tiles=range(T), by_tile=False):
                for t in tiles:
                    if by_tile or t == 0:
                        act.wait_ge(s_ybias, done(b, 1, t))
                    nc.scalar.activation(y[:, t, :], y[:, t, :], ACT.Identity, scale=y_rstd[:, t:t + 1],
                                         bias=y_bias[:, t:t + 1]).then_inc(s_yn, 1)

            def first_audio_hi(c):
                first_hi(audio, c, wa_in, wa_hi, KH + 2, s_cT0, s_cThi, s_wahi)

            for c in range(KH):
                first_hi(text, c, wt_in, wt_hi, 0, s_xT0, s_xThi, s_wthi)
            first_audio_hi(0)
            act.wait_ge(s_wtlo, KH)
            act.wait_ge(s_bcent, 2)
            first_bias(text, 0, B)
            first_bias(text, 1, B)
            first_square(text, 0, squares)
            first_audio_hi(1)
            first_bias(text, 2, B)
            first_square(text, 1, squares)
            first_bias(text, 3, B)
            first_audio_hi(2)
            first_square(text, 2, squares)
            first_square(text, 3, squares)
            act.wait_ge(s_walo, KD)
            act.wait_ge(s_xTlo, KH)
            act.wait_ge(s_const, 4)
            first_bias(audio, 0, A)
            first_bias(audio, 1, A)
            variance(text, 0, B[3])
            first_square(audio, 0, audio_squares0)
            first_bias(audio, 2, A)
            cut_rstd(text, 0)
            first_square(audio, 1, audio_squares0)
            first_bias(audio, 3, A)
            first_square(audio, 2, audio_squares0)
            first_square(audio, 3, audio_squares0)
            variance(audio, 0, A[3])
            affine_chunk(text, 0, 0)
            affine_chunk(text, 0, 1)
            cut_rstd(audio, 0)
            cut_chunk(text, 0, 0)
            cut_chunk(text, 0, 1)
            affine_chunk(text, 0, 2)
            affine_chunk(audio, 0, 0)
            cut_chunk(audio, 0, 0)
            affine_chunk(audio, 0, 1)
            cut_chunk(audio, 0, 1)
            cut_chunk(text, 0, 2)
            affine_chunk(audio, 0, 2)
            cut_chunk(audio, 0, 2)
            affine_chunk(text, 0, 3)
            cut_chunk(text, 0, 3)
            affine_chunk(audio, 0, 3)
            cut_chunk(audio, 0, 3)
            for i in range(KD):
                act.wait_ge(s_wvmm, i + 1)
                nc.scalar.activation(wv_hi[:, i, :], B[i][:, :], ACT.Copy).then_inc(s_wvhi, 1)

            def step(b, first=False, next1=True, next2=True):
                if next1:
                    if not first:
                        act.wait_ge(s_omm, done(b - 1, T, T - 1))
                    cut_cT(b + 1)
                    if first:
                        cut_xT(b + 1, range(KH))
                else:
                    cut_c(b)
                exps(b, (0,) if next1 else (0, 1))
                if not first:
                    norm_y(b - 1, (0, 1))
                exps(b, (1,) if next1 else (2,))
                if not first:
                    norm_y(b - 1, (2, 3))
                exps(b, (2, 3) if next1 else (3,))
                if not next1:
                    probs_hi(b, B)
                else:
                    cut_c(b)
                    square(audio, b + 1, range(KH))
                    probs_hi(b, A)
                    variance(audio, b + 1, A[3])
                    square(text, b + 1, (0,))
                    cut_rstd(audio, b + 1)
                    square(text, b + 1, (1, 2))
                    affine(audio, b + 1, (0, 1))
                    square(text, b + 1, (3,))
                    affine(audio, b + 1, (2, 3, 4))
                probs_ctx_hi(b, 0)
                if next1:
                    variance(text, b + 1, A[3])
                probs_ctx_hi(b, 1)
                if next1:
                    cut_rstd(text, b + 1)
                probs_ctx_hi(b, 2)
                if next1:
                    affine(text, b + 1)
                if next2:
                    cut_xT(b + 2, range(KH))

            step(0, first=True)
            with act.Fori(1, BATCHES - 2) as b:
                step(b)
            step(BATCHES - 2, next2=False)
            step(BATCHES - 1, next1=False, next2=False)
            norm_y(BATCHES - 1, by_tile=True)

        @block.vector
        def _(dve):
            def f(ap):
                return ap.bitcast(f32)

            def row_mean(row, col, landed, landed_at):
                dve.wait_ge(landed, landed_at)
                nc.vector.reduce_sum(w_mean[:, col:col + 1], row, AX.X).then_inc(s_wmean, 1)
                dve.wait_ge(s_wmean, 2 * col + 1)
                nc.vector.tensor_scalar(w_mean[:, col:col + 1], w_mean[:, col:col + 1], -1.0 / H, None,
                                        ALU.mult).then_inc(s_wmean, 1)

            def first_lo(side, w, w_col, w_landed, hi_made, lo_made, w_hi_made, w_lo_made):
                for c in range(side.chunks):
                    col = w_col + c
                    row_mean(w[:, c, :], col, w_landed[c], DMA)
                    dve.wait_ge(hi_made, c + 1)
                    nc.vector.tensor_tensor(side.in_lo[:, c, :], side.inT[:, c, :], f(side.in_hi[:, c, :]),
                                            ALU.subtract).then_inc(lo_made, 1)
                    dve.wait_ge(w_hi_made, c + 1)
                    nc.vector.scalar_tensor_tensor(out=side.w_lo[:, c, :], in0=w[:, c, :],
                                                   scalar=w_mean[:, col:col + 1],
                                                   in1=f(side.w_hi[:, c, :]), op0=ALU.add,
                                                   op1=ALU.subtract).then_inc(w_lo_made, 1)

            def centre_bias(side, row, column, col):
                row_mean(row, col, s_brows, 2 * DMA)
                dve.wait_ge(s_wmean, 2 * col + 2)
                nc.vector.tensor_scalar(bias_cols[:, side.bias, :], cols[:, column, :], w_mean[:, col:col + 1], None,
                                        ALU.add).then_inc(s_bcent, 1)

            def cut_xT(b, chunks):
                for c in chunks:
                    dve.wait_ge(s_xThi, done(b, KH, c))
                    nc.vector.tensor_tensor(xT_lo[:, c, :], xT_in[:, c, :], f(xT_hi[:, c, :]),
                                            ALU.subtract).then_inc(s_xTlo, 1)

            def cut_cT(b):
                for c in range(KD):
                    dve.wait_ge(s_cThi, done(b, KD, c))
                    nc.vector.tensor_tensor(cT_lo[:, c, :], cT_in[:, c, :], f(cT_hi[:, c, :]),
                                            ALU.subtract).then_inc(s_cTlo, 1)

            def cut_c(b, t):
                dve.wait_ge(s_chi, done(b, T, t))
                nc.vector.tensor_tensor(c_lo[:, t, :], c_in[:, t, :], f(c_hi[:, t, :]),
                                        ALU.subtract).then_inc(s_clo, 1)

            def add_bias(side, b, chunks, banks=B):
                for c in chunks:
                    dve.wait_ge(side.product_made, done(b, KH, c))
                    nc.vector.tensor_scalar(side.raw[:, c, :], banks[c][:, :],
                                            bias_cols[:, side.bias, c:c + 1], None,
                                            ALU.add).then_inc(side.biased, 1)

            def add_audio_squares0():
                for c in range(1, KH):
                    dve.wait_ge(audio.squared, c + 1)
                    if c > 1:
                        dve.wait_ge(audio.added, c - 1)
                    nc.vector.tensor_tensor(audio_squares0[:, 0, :], audio_squares0[:, 0, :], audio_squares0[:, c, :],
                                            ALU.add).then_inc(audio.added, 1)

            def fold(side, b, squares=squares):
                u32 = mybir.dt.uint32
                dve.wait_ge(side.added, done(b, KH - 1, KH - 2))
                nc.vector.transpose(squares[:, 1, :].bitcast(u32),
                                    squares[:, 0, :].bitcast(u32)).then_inc(side.fold_made, 1)
                dve.wait_ge(side.fold_made, done(b, 2, 0))
                nc.vector.reduce_sum(side.folded[:, :], squares[:, 1, :].rearrange("p (n i) -> p n i", i=32),
                                     AX.X).then_inc(side.fold_made, 1)

            def diagonals(side, b):
                for diag, column, made in ((diag_hi, side.rstd, side.rstd_made),
                                           (diag_lo, side.rstd_lo, side.rstd_lo_made)):
                    dve.wait_ge(made, done(b, 1, 0))
                    nc.vector.tensor_tensor(diag[:, :, :],
                                            ident[:, :].rearrange("p (o i) -> p o i", o=1).broadcast_to([P, T, P]),
                                            column[:, :].rearrange("p (t o) -> p t o", o=1).broadcast_to([P, T, P]),
                                            ALU.mult).then_inc(side.diag_made, 1)

            def norm(side, b, c, bank=A[3]):
                if c == 0:
                    dve.wait_ge(side.spread, done(b, 1, 0))
                nc.vector.tensor_tensor(side.raw[:, c, :], side.raw[:, c, :], bank[:, :],
                                        ALU.mult).then_inc(side.normed, 1)

            def cut(side, b, c):
                dve.wait_ge(side.hi_made, done(b, KH, c))
                nc.vector.tensor_tensor(side.lo[:, c, :], side.raw[:, c, :], f(side.hi[:, c, :]),
                                        ALU.subtract).then_inc(side.lo_made, 1)

            def score_max(b, t):
                dve.wait_ge(s_smm, done(b, T, t))
                nc.vector.reduce_max(s_max[:, t:t + 1], A[t][:, :], AX.X).then_inc(s_smax, 1)
                dve.wait_ge(s_smax, done(b, T, t))
                nc.vector.tensor_scalar(s_bias[:, t:t + 1], s_max[:, t:t + 1], -SCALE, None,
                                        ALU.mult).then_inc(s_sbias, 1)

            def inverse_sums(b):
                dve.wait_ge(s_exp, done(b, T, T - 1))
                nc.vector.reciprocal(p_inv[:, :], p_sum[:, :]).then_inc(s_pinv, 1)

            def probs_lo(b, banks):
                for j in range(T):
                    dve.wait_ge(s_phi, done(b, T, j))
                    nc.vector.tensor_tensor(pT_lo[:, j, :], banks[j][:, :], f(pT_hi[:, j, :]),
                                            ALU.subtract).then_inc(s_plo, 1)

            def probs_ctx_lo(b, i):
                dve.wait_ge(s_pchi, done(b, KD, i))
                nc.vector.tensor_tensor(pcT_lo[:, i, :], A[i][:, :], f(pcT_hi[:, i, :]),
                                        ALU.subtract).then_inc(s_pclo, 1)

            def scale_and_shift(b, t):
                dve.wait_ge(s_yn, done(b, T, t))
                nc.vector.tensor_tensor(y[:, t, :], y[:, t, :], go_row[:, :], ALU.mult).then_inc(s_yg_last, 1)
                dve.wait_ge(s_yg_last, t)
                nc.vector.tensor_tensor(y[:, t, :], y[:, t, :], be_row[:, :], ALU.add).then_inc(s_yout_last, 1)

            def output_rows(b, t):
                if t == 0:
                    dve.wait_ge(s_pinv, done(b, 1, 0))
                dve.wait_ge(s_xres, done(b, T, t))
                dve.wait_ge(s_omm, done(b, T, t))
                nc.vector.scalar_tensor_tensor(out=y[:, t, :], in0=B[t][:, :], scalar=p_inv[:, t:t + 1],
                                               in1=y[:, t, :], op0=ALU.mult, op1=ALU.add).then_inc(s_y, 1)
                dve.wait_ge(s_y, done(b, T, t))
                nc.vector.bn_stats(y_bn[:, t, :], y[:, t, :]).then_inc(s_ybn, 1)
                dve.wait_ge(s_walo, 1)
                dve.wait_ge(s_ybn, done(b, T, t))
                nc.vector.bn_aggr(y_mv[:, t, :], y_bn[:, t, :]).then_inc(s_ymv, 1)

            dve.wait_ge(s_const, 4)
            nc.vector.tensor_copy(ones[:, :], consts[:, ONE, 0:1].broadcast_to([P, P])).then_inc(s_ones, 1)
            dve.wait_ge(s_const, 5)
            same = same_of_32[:, :].rearrange("p (g i) -> p g i", i=32)
            nc.vector.reduce_sum(same[:, 0, :], ident[:, :].rearrange("p (g i) -> p i g", i=32),
                                 AX.X).then_inc(s_same, 1)
            dve.wait_ge(s_same, 1)
            nc.vector.tensor_copy(same[:, 1:4, :], same[:, 0:1, :].broadcast_to([P, 3, 32])).then_inc(s_same, 1)
            dve.wait_ge(s_same, 2)
            first_lo(text, wt_in, 0, s_wt, s_xThi, s_xTlo, s_wthi, s_wtlo)
            dve.wait_ge(s_cols, 6 * DMA)
            centre_bias(text, bt_row, BT, KH)
            centre_bias(audio, ba_row, BA, KH + 1)
            nc.vector.tensor_copy(ba_cols, cols[:, BA, :].rearrange("p (c o) -> p c o", o=1)
                                  .broadcast_to([P, KH, P])).then_inc(s_bacols, 1)
            first_lo(audio, wa_in, KH + 2, s_wa, s_cThi, s_cTlo, s_wahi, s_walo)
            fold(text, 0)
            diagonals(text, 0)
            add_audio_squares0()
            fold(audio, 0, audio_squares0)
            norm(text, 0, 0, B[3])
            norm(text, 0, 1, B[3])
            norm(text, 0, 2, B[3])
            diagonals(audio, 0)
            norm(text, 0, 3, B[3])
            norm(audio, 0, 0)
            norm(audio, 0, 1)
            cut(audio, 0, 0)
            norm(audio, 0, 2)
            dve.wait_ge(s_rows, 3 * DMA)
            dve.wait_ge(s_resmm, 1)
            nc.vector.tensor_tensor(res_row[:, :], A[0][:, :], res_row[:, :], ALU.add).then_inc(s_res, 1)
            cut(audio, 0, 1)
            norm(audio, 0, 3)
            cut(audio, 0, 2)
            cut(audio, 0, 3)
            for i in range(KD):
                dve.wait_ge(s_wvhi, i + 1)
                nc.vector.tensor_tensor(wv_lo[:, i, :], B[i][:, :], f(wv_hi[:, i, :]),
                                        ALU.subtract).then_inc(s_wvlo, 1)

            def step(b, first=False, next1=True):
                if first:
                    cut_cT(b + 1)
                score_max(b, 0)
                if next1:
                    if not first:
                        cut_cT(b + 1)
                    cut_xT(b + 1, (0, 1))
                score_max(b, 1)
                if next1:
                    cut_xT(b + 1, (2, 3))
                else:
                    for t in range(T):
                        cut_c(b, t)
                score_max(b, 2)
                score_max(b, 3)
                inverse_sums(b)
                if next1:
                    for t in range(T):
                        add_bias(audio, b + 1, (t,))
                        cut_c(b, t)
                    probs_lo(b, A)
                else:
                    probs_lo(b, B)
                if next1:
                    add_bias(text, b + 1, (0,))
                    fold(audio, b + 1)
                    add_bias(text, b + 1, (1,))
                    diagonals(audio, b + 1)
                    add_bias(text, b + 1, (2,))
                    norm(audio, b + 1, 0)
                    norm(audio, b + 1, 1)
                    norm(audio, b + 1, 2)
                    add_bias(text, b + 1, (3,))
                    norm(audio, b + 1, 3)
                    cut(audio, b + 1, 0)
                    fold(text, b + 1)
                    for c in range(1, KH):
                        cut(audio, b + 1, c)
                probs_ctx_lo(b, 0)
                if next1:
                    diagonals(text, b + 1)
                probs_ctx_lo(b, 1)
                probs_ctx_lo(b, 2)
                if next1:
                    for c in range(KH):
                        norm(text, b + 1, c)
                    cut(text, b + 1, 0)
                    output_rows(b, 0)
                    cut(text, b + 1, 1)
                    cut(text, b + 1, 2)
                    output_rows(b, 1)
                    cut(text, b + 1, 3)
                    output_rows(b, 2)
                    output_rows(b, 3)
                else:
                    for t in range(T):
                        output_rows(b, t)
                    for t in range(1, T):
                        scale_and_shift(b, t)

            step(0, first=True)
            with dve.Fori(1, BATCHES - 1) as b:
                step(b)
            step(BATCHES - 1, next1=False)

        @block.gpsimd
        def _(pool):
            nc.gpsimd.memset(ident[:, :], 0.0).then_inc(s_ident0, 1)
            for const, value in ((MINUS_HALF, -0.5), (EPSILON, EPS), (ZERO, 0.0), (ONE, 1.0)):
                nc.gpsimd.memset(consts[:, const, :], value).then_inc(s_const, 1)
            pool.wait_ge(s_ident0, 1)
            nc.gpsimd.affine_select(out=ident[:, :], in_=ident[:, :], compare_op=ALU.not_equal, fill=1.0,
                                    base=0, pattern=[[-1, P]], channel_multiplier=1).then_inc(s_const, 1)
            for row, v in ((ba_row, b_audio), (bt_row, b_text)):
                pool.dma_start(row, v.rearrange("(a h) -> a h", a=1).partition_broadcast(P)).then_inc(s_brows, DMA)
            for i, v in enumerate((g1, beta1, g2, beta2, b_audio_col, b_text_col)):
                pool.dma_start(cols[:, i, :], v).then_inc(s_cols, DMA)
            pool.dma_start(waT_in, w_audio_t.rearrange("(c p) d -> p c d", p=P)).then_inc(s_waT, DMA)
            pool.dma_start(wo_in, w_out.rearrange("(c p) h -> p c h", p=P)).then_inc(s_wo, DMA)
            for row, v in ((res_row, b_out), (go_row, g_out), (be_row, beta_out)):
                pool.dma_start(row[:, :], v.rearrange("(a h) -> a h", a=1).partition_broadcast(P)).then_inc(s_rows, DMA)

            def add_squares(side, b):
                for c in range(1, KH):
                    pool.wait_ge(side.squared, done(b, KH, c))
                    if c > 1:
                        pool.wait_ge(side.added, done(b, KH - 1, c - 2))
                    nc.gpsimd.tensor_tensor(squares[:, 0, :], squares[:, 0, :], squares[:, c, :],
                                            ALU.add).then_inc(side.added, 1)

            def inverse_deviation(side, b):
                pool.wait_ge(side.var_made, done(b, 4, 3))
                nc.gpsimd.tensor_tensor(side.rstd[:, :], side.var[:, :], consts[:, MINUS_HALF, :],
                                        ALU.pow).then_inc(side.rstd_made, 1)
                pool.wait_ge(side.rstd_hi_made, done(b, 1, 0))
                nc.gpsimd.tensor_tensor(side.rstd_lo[:, :], side.rstd[:, :], side.rstd_hi[:, :].bitcast(f32),
                                        ALU.subtract).then_inc(side.rstd_lo_made, 1)

            def add_residual(b):
                for t in range(T):
                    pool.wait_ge(s_xin[t], DMA * (b + 1))
                    nc.gpsimd.tensor_tensor(y[:, t, :], y[:, t, :], res_row[:, :], ALU.add).then_inc(s_xres, 1)

            def norms(b, n, t):
                nc.gpsimd.tensor_tensor(y_var[:, t], y_mv[:, t, 1], consts[:, EPSILON, t], ALU.add).then_inc(s_yvar, 1)
                pool.wait_ge(s_yvar, done(b, 1, n))
                nc.gpsimd.tensor_tensor(y_rstd[:, t], y_var[:, t], consts[:, MINUS_HALF, t],
                                        ALU.pow).then_inc(s_yrs, 1)
                pool.wait_ge(s_yrs, done(b, 1, n))
                nc.gpsimd.tensor_tensor(y_mr[:, t], y_mv[:, t, 0], y_rstd[:, t], ALU.mult).then_inc(s_ymr, 1)
                pool.wait_ge(s_ymr, done(b, 1, n))
                nc.gpsimd.tensor_tensor(y_bias[:, t], consts[:, ZERO, t], y_mr[:, t],
                                        ALU.subtract).then_inc(s_ybias, 1)

            def scale_and_shift(b, t):
                pool.wait_ge(s_yn, done(b, T, t))
                nc.gpsimd.tensor_tensor(y[:, t, :], y[:, t, :], go_row[:, :], ALU.mult).then_inc(s_yg, 1)
                pool.wait_ge(s_yg, done(b, T, t))
                nc.gpsimd.tensor_tensor(y[:, t, :], y[:, t, :], be_row[:, :], ALU.add).then_inc(s_yout, 1)

            def finish(b):
                pool.wait_ge(s_ymv, done(b, T, T - 1))
                norms(b, 0, slice(0, T))
                for t in range(T):
                    scale_and_shift(b, t)

            def finish_last(b):
                for t in range(T):
                    pool.wait_ge(s_ymv, done(b, T, t))
                    norms(b, t, slice(t, t + 1))
                scale_and_shift(b, 0)

            pool.wait_ge(s_const, 5)
            add_squares(text, 0)
            inverse_deviation(text, 0)
            inverse_deviation(audio, 0)
            for c in range(KH):
                pool.wait_ge(text.hi_made, c + 1)
                nc.gpsimd.tensor_tensor(qT_lo[:, c, :], q_raw[:, c, :], qT_hi[:, c, :].bitcast(f32),
                                        ALU.subtract).then_inc(text.lo_made, 1)
            pool.wait_ge(s_res, 1)

            def step(b, first=False, next1=True):
                if not first:
                    finish(b - 1)
                if next1:
                    add_squares(audio, b + 1)
                    inverse_deviation(audio, b + 1)
                    add_squares(text, b + 1)
                    inverse_deviation(text, b + 1)
                add_residual(b)

            step(0, first=True)
            with pool.Fori(1, BATCHES - 1) as b:
                step(b)
            step(BATCHES - 1, next1=False)
            finish_last(BATCHES - 1)


def kernel(**inputs):
    import numpy as _np
    import concourse.bacc as _bacc
    from concourse import mybir as _mybir
    from concourse.bass_utils import run_bass_kernel_spmd as _run

    P = 128
    x = _np.asarray(inputs["x"])
    c = _np.asarray(inputs["ctx_768"])

    def rows(a):
        n, r, d = a.shape
        return a.reshape(n, P, (r // P) * d)

    def columns(a):
        n, r, d = a.shape
        return a.reshape(n, P, r // P, d // P, P).transpose(0, 4, 3, 2, 1).reshape(n, P, (d // P) * r)

    def column(v):
        return v.reshape(-1, P).T

    w = {k.removeprefix("L0_xattn_"): _np.asarray(v) for k, v in inputs.items()}
    given = {
        "x_rows": rows(x), "x_cols": columns(x), "ctx_rows": rows(c), "ctx_cols": columns(c),
        "w_text": w["W_text"], "b_text": w["b_text"], "w_audio": w["W_audio"], "w_audio_t": w["W_audio"].T,
        "b_audio": w["b_audio"], "w_out": w["W_out"], "b_out": w["b_out"],
        "g1": column(w["g1"]), "beta1": column(w["beta1"]), "g2": column(w["g2"]), "beta2": column(w["beta2"]),
        "b_audio_col": column(w["b_audio"]), "b_text_col": column(w["b_text"]),
        "g_out": w["g_out"], "beta_out": w["beta_out"],
    }
    nc = _bacc.Bacc("TRN2", target_bir_lowering=False, num_devices=1)
    arrays, aps = {}, {}
    for name, a in given.items():
        a = _np.ascontiguousarray(a)
        arrays[f"in_{name}"] = a
        aps[name] = nc.dram_tensor(f"in_{name}", a.shape, _mybir.dt.from_np(a.dtype), kind="ExternalInput").ap()
    n, r, d = x.shape
    aps["out"] = nc.dram_tensor("out_rows", (n, P, (r // P) * d), _mybir.dt.float32, kind="ExternalOutput").ap()
    cross_attention(nc, **aps)
    res = _run(nc, [arrays], core_ids=[0])
    return res.results[0]["out_rows"].reshape(n, r, d)
```
